# Optimizing a Trainium2 kernel written in Bass

```python
import numpy as np
import jax
import jax.numpy as jnp

def _softmax(x, axis=-1):
    return jax.nn.softmax(x, axis=axis)

def _gelu(x):
    return jax.nn.gelu(x, approximate=True)

def _silu(x):
    return jax.nn.silu(x)

def _sigmoid(x):
    return jax.nn.sigmoid(x)

def _layernorm(x, axis=-1, eps=1e-05):
    m = jnp.mean(x, axis=axis, keepdims=True)
    v = jnp.var(x, axis=axis, keepdims=True)
    return (x - m) / jnp.sqrt(v + eps)

def _scatter_add(tgt, idx, src, axis=0):
    return tgt.at[idx].add(src)

def _segment_sum(src, seg, n):
    return jax.ops.segment_sum(src, seg, n)
kernel_name = 'mk_decoder_preln_d1_seqx_r8_0d26a7'

def setup_inputs(seed: int=0):
    np.random.seed(seed)
    _w = jnp.asarray

    def _rec_inputs():
        import jax
        import jax.numpy as jnp
        _rk = jax.random.key(seed)
        x = 7.22e-05 + 1 * jax.random.normal(jax.random.fold_in(_rk, 1), (4, 256, 256), jnp.float32)
        _lenS = 256 - jax.random.randint(jax.random.fold_in(_rk, 7), (4,), 0, max(1, 256 // 4) + 1, jnp.int32)
        _lenS2 = 256 - jax.random.randint(jax.random.fold_in(_rk, 8), (4,), 0, max(1, 256 // 4) + 1, jnp.int32)
        _ctx_1024P = jax.random.normal(jax.random.fold_in(_rk, 11), (4, 16, 128), jnp.float32)
        _ctx_1024c = jax.random.dirichlet(jax.random.fold_in(_rk, 511), 0.3 * jnp.ones((16,), jnp.float32), (4, 256))
        _ctx_1024t = jnp.einsum('bsk,bkd->bsd', _ctx_1024c, _ctx_1024P)
        _ctx_1024t = _ctx_1024t * jax.lax.rsqrt(jnp.mean(jnp.square(_ctx_1024t)) + 1e-12) * 0.953939
        ctx_1024 = 2.81802e-05 + 1.00001 * (_ctx_1024t + 0.3 * jax.random.normal(jax.random.fold_in(_rk, 611), (4, 256, 128), jnp.float32))
        return (x, ctx_1024)
    x, ctx_1024 = _rec_inputs()

    def _L0_attn_setup():
        import jax, jax.numpy as jnp
        import numpy as np
        HID = 256
        HEADS = 16
        HD = HID // HEADS
        EPS = 1e-06

        def _heads(x, b, s):
            return x.reshape(b, s, HEADS, HD).transpose(0, 2, 1, 3)
        key = jax.random.key(seed)
        ks = jax.random.split(key, 9)
        s = 1.0 / np.sqrt(HID)
        return {'hidden_states': jax.random.normal(ks[0], (4, 512, HID), jnp.float32), 'q_w': jax.random.normal(ks[1], (HID, HID), jnp.float32) * s, 'q_b': jnp.zeros((HID,), jnp.float32), 'k_w': jax.random.normal(ks[2], (HID, HID), jnp.float32) * s, 'k_b': jnp.zeros((HID,), jnp.float32), 'v_w': jax.random.normal(ks[3], (HID, HID), jnp.float32) * s, 'v_b': jnp.zeros((HID,), jnp.float32), 'o_w': jax.random.normal(ks[4], (HID, HID), jnp.float32) * s, 'o_b': jnp.zeros((HID,), jnp.float32)}
    _L0_attn_all = _L0_attn_setup()
    _L0_attn_in = {k: v for k, v in _L0_attn_all.items() if k in ('q_w', 'q_b', 'k_w', 'k_b', 'v_w', 'v_b', 'o_w', 'o_b')}
    del _L0_attn_all

    def _L0_xattn_setup():
        import jax, jax.numpy as jnp
        import numpy as np
        key = jax.random.key(seed)
        ks = jax.random.split(key, 6)
        B, L, N, C, D = (8, 64, 256, 128, 128)
        return {'teacher_logits': jax.random.normal(ks[0], (B, L, N), dtype=jnp.float32), 'teacher_features': jax.random.normal(ks[1], (B, N, C), dtype=jnp.float32), 'Wq': jax.random.normal(ks[2], (D, C), dtype=jnp.float32) * (1.0 / np.sqrt(C)), 'bq': jnp.zeros((D,), dtype=jnp.float32), 'Wk': jax.random.normal(ks[3], (D, C), dtype=jnp.float32) * (1.0 / np.sqrt(C)), 'bk': jnp.zeros((D,), dtype=jnp.float32)}
    _L0_xattn_all = _L0_xattn_setup()
    _L0_xattn_in = {k: v for k, v in _L0_xattn_all.items() if k in ('Wq', 'bq', 'Wk', 'bk')}
    del _L0_xattn_all

    def _L0_ffn_setup():
        import jax, jax.numpy as jnp
        import numpy as np
        B, S, D, H = (4, 256, 256, 1024)

        def fwht(x):
            orig_shape = x.shape
            n = orig_shape[-1]
            x = x.reshape(-1, n)
            h = 1
            while h < n:
                xb = x.reshape(-1, n // (2 * h), 2, h)
                a = xb[:, :, 0, :]
                b = xb[:, :, 1, :]
                x = jnp.stack([a + b, a - b], axis=2).reshape(-1, n)
                h *= 2
            scale = jnp.asarray(1.0 / np.sqrt(n), dtype=x.dtype)
            return (x * scale).reshape(orig_shape)
        key = jax.random.key(seed)
        kx, k1, k2, k3 = jax.random.split(key, 4)
        x = jax.random.normal(kx, (B, S, D), dtype=jnp.float32)
        W1 = jax.random.normal(k1, (H, D), dtype=jnp.float32) * (1.0 / np.sqrt(D))
        W2 = jax.random.normal(k2, (D, H), dtype=jnp.float32) * (1.0 / np.sqrt(H))
        W3 = jax.random.normal(k3, (H, D), dtype=jnp.float32) * (1.0 / np.sqrt(D))
        return {'x': x, 'W1': W1, 'W2': W2, 'W3': W3}
    _L0_ffn_all = _L0_ffn_setup()
    _L0_ffn_in = {k: v for k, v in _L0_ffn_all.items() if k in ('W1', 'W2', 'W3')}
    del _L0_ffn_all
    return {'x': x, 'ctx_1024': ctx_1024, 'L0_attn_q_w': _L0_attn_in['q_w'], 'L0_attn_q_b': _L0_attn_in['q_b'], 'L0_attn_k_w': _L0_attn_in['k_w'], 'L0_attn_k_b': _L0_attn_in['k_b'], 'L0_attn_v_w': _L0_attn_in['v_w'], 'L0_attn_v_b': _L0_attn_in['v_b'], 'L0_attn_o_w': _L0_attn_in['o_w'], 'L0_attn_o_b': _L0_attn_in['o_b'], 'L0_xattn_Wq': _L0_xattn_in['Wq'], 'L0_xattn_bq': _L0_xattn_in['bq'], 'L0_xattn_Wk': _L0_xattn_in['Wk'], 'L0_xattn_bk': _L0_xattn_in['bk'], 'L0_ffn_W1': _L0_ffn_in['W1'], 'L0_ffn_W2': _L0_ffn_in['W2'], 'L0_ffn_W3': _L0_ffn_in['W3']}

def reference(x, ctx_1024, L0_attn_q_w, L0_attn_q_b, L0_attn_k_w, L0_attn_k_b, L0_attn_v_w, L0_attn_v_b, L0_attn_o_w, L0_attn_o_b, L0_xattn_Wq, L0_xattn_bq, L0_xattn_Wk, L0_xattn_bk, L0_ffn_W1, L0_ffn_W2, L0_ffn_W3):
    import jax
    import jax.numpy as jnp

    def _L0_attn_ref(hidden_states, q_w, q_b, k_w, k_b, v_w, v_b, o_w, o_b):
        import jax, jax.numpy as jnp
        import numpy as np
        HID = 256
        HEADS = 16
        HD = HID // HEADS
        EPS = 1e-06

        def _heads(x, b, s):
            return x.reshape(b, s, HEADS, HD).transpose(0, 2, 1, 3)
        b, s, _ = hidden_states.shape
        q = _heads(hidden_states @ q_w.T + q_b, b, s)
        k = _heads(hidden_states @ k_w.T + k_b, b, s)
        v = _heads(hidden_states @ v_w.T + v_b, b, s)
        qp = jax.nn.elu(q) + 1.0
        kp = jax.nn.elu(k) + 1.0
        kv = jnp.einsum('bhsd,bhse->bhde', kp, v)
        z = jnp.einsum('bhsd,bhd->bhs', qp, kp.sum(axis=2))[..., None]
        attn = jnp.einsum('bhsd,bhde->bhse', qp, kv) / (z + EPS)
        out = attn.transpose(0, 2, 1, 3).reshape(b, s, HID)
        return out @ o_w.T + o_b

    def _L0_xattn_ref(teacher_logits, teacher_features, Wq, bq, Wk, bk):
        import jax, jax.numpy as jnp
        import numpy as np
        query = jnp.einsum('bnc,dc->bnd', teacher_features, Wq) + bq
        key = jnp.einsum('bnc,dc->bnd', teacher_features, Wk) + bk
        energy = jnp.einsum('bnd,bmd->bnm', query, key)
        attention = jax.nn.softmax(energy, axis=-1)
        x_m = jnp.einsum('bln,bmn->blm', teacher_logits, attention)
        return x_m

    def _L0_ffn_ref(x, W1, W2, W3):
        import jax, jax.numpy as jnp
        import numpy as np
        B, S, D, H = (4, 256, 256, 1024)

        def fwht(x):
            orig_shape = x.shape
            n = orig_shape[-1]
            x = x.reshape(-1, n)
            h = 1
            while h < n:
                xb = x.reshape(-1, n // (2 * h), 2, h)
                a = xb[:, :, 0, :]
                b = xb[:, :, 1, :]
                x = jnp.stack([a + b, a - b], axis=2).reshape(-1, n)
                h *= 2
            scale = jnp.asarray(1.0 / np.sqrt(n), dtype=x.dtype)
            return (x * scale).reshape(orig_shape)
        up_gate = jnp.einsum('bsd,hd->bsh', x, W1)
        up_lin = jnp.einsum('bsd,hd->bsh', x, W3)
        hidden = jax.nn.silu(up_gate) * up_lin
        hidden = fwht(hidden)
        out = jnp.einsum('bsh,dh->bsd', hidden, W2)
        return out
    x = x + _L0_attn_ref(_layernorm(x, axis=-1), L0_attn_q_w, L0_attn_q_b, L0_attn_k_w, L0_attn_k_b, L0_attn_v_w, L0_attn_v_b, L0_attn_o_w, L0_attn_o_b)
    x = x + _L0_xattn_ref(_layernorm(x, axis=-1), ctx_1024, L0_xattn_Wq, L0_xattn_bq, L0_xattn_Wk, L0_xattn_bk)
    x = x + _L0_ffn_ref(_layernorm(x, axis=-1), L0_ffn_W1, L0_ffn_W2, L0_ffn_W3)
    return x

_drawn_inputs = setup_inputs


def setup_inputs(seed=0):
    import zlib

    import numpy as np

    out = dict(_drawn_inputs(seed))
    spreads = {'L0_attn_q_b': (0.0, 0.8),
     'L0_attn_k_b': (0.0, 0.8),
     'L0_attn_v_b': (0.0, 0.1),
     'L0_attn_o_b': (0.0, 0.1),
     'L0_xattn_bq': (0.0, 0.1),
     'L0_xattn_bk': (0.0, 0.8)}
    factors = {'L0_attn_q_w': 5.236, 'L0_attn_k_w': 2.993}
    for name, (base, spread) in spreads.items():
        noise = np.random.default_rng([zlib.crc32(name.encode()), seed]).standard_normal(out[name].shape)
        drawn = base * np.exp(spread * noise) if base else spread * noise
        out[name] = jnp.asarray(drawn.astype(out[name].dtype))
    for name, factor in factors.items():
        out[name] = (out[name] * factor).astype(out[name].dtype)
    return out
```

```python
import concourse.bass as bass
from concourse import mybir
from contextlib import ExitStack


def decoder_layer(nc, x, ctxT, q_wT, k_wT, v_wT, o_wT, xq_wT, xk_wT, w1T, w3T, w2T,
                  q_b, xq_b, xk_b, k_b, v_b, o_b, consts, out):
    f32, f32r, i32 = mybir.dt.float32, mybir.dt.float32r, mybir.dt.int32
    ALU, ACT, AX = mybir.AluOpType, mybir.ActivationFunctionType, mybir.AxisListType

    P = 128
    TOK, D = x.shape
    T = TOK // P
    B = 4
    S = TOK // B
    G, TG = 2, T // 2
    N = TG * P
    K = D // P
    HD = 16
    HC = P // HD
    H = w1T.shape[1]
    J = H // P
    LN_EPS, Z_EPS = 1e-5, 1e-6
    RSQRT_SEED = 0x5F3759DF
    HAD_SCALE = 1.0 / float(H) ** 0.5
    PARTS = ((1, 0), (0, 1), (0, 0))

    tiles = lambda ap: ap.rearrange("(t p) c -> p t c", p=P)

    ctx = ExitStack()
    with ctx:
        def sb(name, shape, dt=f32):
            return ctx.enter_context(nc.sbuf_tensor(name, shape, dt))

        def sem(name):
            return ctx.enter_context(nc.semaphore(name))

        res = sb("res", [P, T, D])
        ln = sb("ln", [P, T, D])
        lnT = [sb("lnT_hi", [P, G, K, N], f32r), sb("lnT_lo", [P, G, K, N], f32r)]
        colT = sb("colT", [P, G, K, N])
        qp = sb("qp", [P, G, K, N])
        eq = sb("eq", [P, K, N])
        KVW = P + 1
        kvs = sb("kvs", [P, T, 2 * K, KVW])
        ctx_sb = sb("ctx_sb", [P, TOK])
        ek = ctx_sb[:, :].rearrange("p (t c) -> p t c", c=D)
        wqkv = [sb("wqkv_hi", [P, K, 3 * D], f32r), sb("wqkv_lo", [P, K, 3 * D], f32r)]
        wqkv_raw = kvs[:, :, :, :].rearrange("p t c w -> p (t c w)")[:, 0:K * 3 * D].rearrange(
            "p (k n) -> p k n", k=K)
        wo = sb("wo", [P, K, D])
        wxq = sb("wxq", [P, 2, P])
        xqk = sb("xqk", [P, B, 2, S])
        att = xqk
        attT = sb("attT", [P, B, K, S])
        w13_raw = sb("w13_raw", [P, 2, H])
        w13 = [sb("w13_hi", [P, 2, K, H], f32r), sb("w13_lo", [P, 2, K, H], f32r)]
        w2a = sb("w2a", [P, J, D])
        w2b = sb("w2b", [P, J, D])
        w2s = [sb("w2s_hi", [P, 2, D], f32r), sb("w2s_lo", [P, 2, D], f32r)]
        w2 = [sb("w2_hi", [P, J, D], f32r), sb("w2_lo", [P, J, D], f32r)]
        kvx = sb("kvx", [P, B, K, P + HC])
        gated = qp[:, 0, :, :]
        hid = qp[:, 1, :, :]
        hs = [sb("hid_hi", [P, 3, N], f32r), sb("hid_lo", [P, 3, N], f32r)]
        kvb = sb("kvb", [P, 2 * D])
        ob = sb("ob", [P, D])
        qb = sb("qb", [P, K])
        qb1 = sb("qb1", [P, K])
        xqb = sb("xqb", [P, 2])
        cst = sb("cst", [P, 2 * P + P + HC])
        ident, had, headmask = cst[:, 0:P], cst[:, P:2 * P], cst[:, 2 * P:3 * P]
        headcols = cst[:, 3 * P:3 * P + HC]
        had_r = sb("had_r", [P, P], f32r)
        qbn = sb("qbn", [P, K])
        one = sb("one", [P, 1])
        stats = sb("stats", [P, TG, 6])
        mv = sb("mv", [P, TG, 2])
        ve = sb("ve", [P, TG])
        nt = sb("nt", [P, TG])
        rstd = sb("rstd", [P, TG])
        nmx = sb("nmx", [P, B, 2])
        sums = sb("sums", [P, B, 2])
        rsum = sb("rsum", [P, B, 2])
        zs = sb("zs", [P, K, HC])
        rz = sb("rz", [P, K, HC])

        bank = [ctx.enter_context(nc.psum_tensor(f"bank{i}", [P, 512], f32)) for i in range(8)]
        ring_at = {"wide": 0, "up": 0, "late": 0}
        RINGS = {"wide": (0, 1, 2, 3, 4, 5, 6, 7), "up": (0, 1, 2), "late": (3, 4, 5)}
        ACC = (6, 7)
        where = {}
        before = {}
        last_in = [None] * 8

        def place(unit, ring):
            b = RINGS[ring][ring_at[ring] % len(RINGS[ring])] if isinstance(ring, str) else ring
            if isinstance(ring, str):
                ring_at[ring] += 1
            where[unit], before[unit], last_in[b] = b, last_in[b], unit

        DMA_NAMES = ("x0", "x1", "consts", "ctx", "wxq", "wxk", "qw", "kw", "vw", "w2", "ow", "w10", "w11",
                     "w30", "w31", "qb", "xqb", "xkb", "kb", "vb", "ob")
        loaded = {n: sem("loaded_" + n) for n in DMA_NAMES}
        mm = {n: sem("mm_" + n) for n in ("xqk", "lnT0", "lnT1", "lnT2", "energy", "q", "kv", "kvm", "attn",
                                          "aT", "attT", "o", "xm", "w2h", "gate", "lin", "down")}
        chain = sem("dve_chain")
        normed = [sem(f"normed{i}") for i in range(3)]
        turned_hi = {0: sem("ln1T_hi"), 2: sem("ln3T_hi")}
        turned_lo = {0: sem("ln1T_lo"), 2: sem("ln3T_lo")}
        turned2 = sem("ln2T")
        xqk_done = sem("xqk_done")
        max_done = sem("max_done")
        exp_done = sem("exp_done")
        att_done = sem("att_done")
        attT_done = sem("attT_done")
        q_clamped = sem("q_clamped")
        k_clamped = sem("k_clamped")
        q_exp = sem("q_exp")
        q_done = sem("q_done")
        kv_done = sem("kv_done")
        k_exp = sem("k_exp")
        k_done = sem("k_done")
        kvx_done = sem("kvx_done")
        attn_done = sem("attn_done")
        aT_done = sem("aT_done")
        xob_done = sem("xob_done")
        x1_done = sem("x1_done")
        x2_done = sem("x2_done")
        ready = sem("ready")
        wqkv_hi = sem("wqkv_hi_done")
        wqkv_lo = sem("wqkv_lo_done")
        w13_hi = sem("w13_hi_done")
        w13_lo = sem("w13_lo_done")
        fly = sem("w2_butterfly")
        w2s_hi = sem("w2s_hi_done")
        w2s_lo = sem("w2s_lo_done")
        w2_hi = sem("w2_hi_done")
        w2_lo = sem("w2_lo_done")
        silu_done = sem("silu_done")
        hid_done = sem("hid_done")
        hid_hi = sem("hid_hi_done")
        hid_lo = sem("hid_lo_done")
        out_done = sem("out_done")
        stored = sem("stored")

        def emptied(unit):
            kind, n = unit
            return {"xqk": xqk_done, "lnT0": turned_lo[0], "lnT1": turned2, "lnT2": turned_lo[2],
                    "energy": exp_done, "q": q_exp, "kv": kv_done, "kvm": kvx_done, "attn": attn_done,
                    "aT": aT_done, "attT": attT_done, "o": x1_done, "xm": x2_done, "w2h": w2_lo,
                    "gate": silu_done, "lin": hid_done, "acc": out_done}[kind], n + 1

        EARLY = ([("xqk", i) for i in range(4)] + [("lnT0", 0), ("lnT0", 1), ("energy", 0), ("energy", 1),
                 ("q", 0), ("q", 1)] + [("kv", i) for i in range(4)] + [("energy", 2), ("energy", 3)]
                 + [("lnT0", 2), ("lnT0", 3), ("attT", 0), ("attT", 1), ("kvm", 0), ("kvm", 1), ("q", 2), ("q", 3)]
                 + [("attn", i) for i in range(4)] + [("kv", i) for i in range(4, 8)] + [("aT", 0), ("aT", 1)]
                 + [("attT", 2), ("attT", 3), ("o", 0), ("o", 1), ("kvm", 2), ("kvm", 3)]
                 + [("attn", i) for i in range(4, 8)] + [("lnT1", 0), ("lnT1", 1), ("w2h", 0), ("w2h", 1), ("aT", 2), ("aT", 3)]
                 + [("xm", 0), ("xm", 1), ("o", 2), ("o", 3), ("w2h", 2), ("w2h", 3), ("lnT2", 0), ("lnT2", 1)])
        for unit in EARLY:
            place(unit, "wide")
        for g in range(G):
            for j in range(J):
                place(("gate", g * J + j), "up")
                place(("lin", g * J + j), "up")
            for i in range(2):
                place(("acc", 2 * g + i), ACC[i])
        for unit in (("lnT1", 2), ("lnT1", 3), ("xm", 2), ("xm", 3), ("lnT2", 2), ("lnT2", 3)):
            place(unit, "late")

        block = ctx.enter_context(nc.Block())

        @block.sync
        def _(sp):
            def load(name, dst, src):
                sp.dma_start(dst, src).then_inc(loaded[name], 16)

            xt = tiles(x)
            load("x0", res[:, 0:TG, :], xt[:, 0:TG, :])
            load("qw", wqkv_raw[:, :, 0:D], q_wT.rearrange("(k p) n -> p k n", p=P))
            load("kw", wqkv_raw[:, :, D:2 * D], k_wT.rearrange("(k p) n -> p k n", p=P))
            load("vw", wqkv_raw[:, :, 2 * D:3 * D], v_wT.rearrange("(k p) n -> p k n", p=P))
            load("x1", res[:, TG:T, :], xt[:, TG:T, :])
            load("w2", w2a[:, :, :], w2T.rearrange("(j p) d -> p j d", p=P))
            load("ow", wo[:, :, :], o_wT.rearrange("(k p) n -> p k n", p=P))
            for i, (m, w) in enumerate((("w1", w1T), ("w3", w3T))):
                for k in range(K):
                    n = 2 * i + k
                    if n >= 2:
                        sp.wait_ge(w13_lo, n - 1)
                        sp.wait_ge(w13_hi, n - 1)
                    load(f"{m}{k}", w13_raw[:, n % 2, :], w[k * P:(k + 1) * P, :])
            ot = tiles(out)
            for n in range(2 * G):
                sp.wait_ge(out_done, n + 1)
                sp.dma_start(ot[:, 2 * n:2 * n + 2, :], res[:, 2 * n:2 * n + 2, :]).then_inc(stored, 16)
            sp.wait_ge(stored, 2 * G * 16)

        @block.gpsimd
        def _(pool):
            for i, n in enumerate(("qw", "kw", "vw")):
                pool.wait_ge(loaded[n], 16)
                pool.wait_ge(wqkv_hi, i + 1)
                s = slice(i * D, (i + 1) * D)
                nc.gpsimd.tensor_tensor(wqkv[1][:, :, s], wqkv_raw[:, :, s], wqkv[0][:, :, s],
                                        ALU.subtract).then_inc(wqkv_lo, 1)
            pool.wait_ge(loaded["ob"], 16)

            def residual_bias(g):
                pool.wait_ge(normed[0], TG * (g + 1))
                half = res[:, g * TG:(g + 1) * TG, :]
                nc.gpsimd.tensor_tensor(half, half, ob[:, :].unsqueeze(1).to_broadcast([P, TG, D]),
                                        ALU.add).then_inc(xob_done, 1)

            residual_bias(0)
            pool.wait_ge(loaded["w2"], 16)
            src, dst = w2a, w2b
            for s, step in enumerate((1, 2, 4)):
                if s:
                    pool.wait_ge(fly, 2 * s)
                a = src[:, :, :].rearrange("p (u two v) d -> p u two (v d)", two=2, v=step)
                o = dst[:, :, :].rearrange("p (u two v) d -> p u two (v d)", two=2, v=step)
                nc.gpsimd.tensor_tensor(o[:, :, 0, :], a[:, :, 0, :], a[:, :, 1, :], ALU.add).then_inc(fly, 1)
                nc.gpsimd.tensor_tensor(o[:, :, 1, :], a[:, :, 0, :], a[:, :, 1, :], ALU.subtract).then_inc(fly, 1)
                src, dst = dst, src
                if s == 0:
                    residual_bias(1)
            for n in range(4):
                pool.wait_ge(w2s_hi, n + 1)
                if n:
                    pool.wait_ge(mm["w2h"], n)
                nc.gpsimd.tensor_tensor(w2s[1][:, :, :], w2b[:, 2 * n:2 * n + 2, :], w2s[0][:, :, :],
                                        ALU.subtract).then_inc(w2s_lo, 1)
                if n in (0, 2):
                    for m in (n, n + 1):
                        pool.wait_ge(loaded[("w10", "w11", "w30", "w31")[m]], 16)
                        pool.wait_ge(w13_hi, m + 1)
                        nc.gpsimd.tensor_tensor(w13[1][:, m // 2, m % 2, :], w13_raw[:, m % 2, :],
                                                w13[0][:, m // 2, m % 2, :], ALU.subtract).then_inc(w13_lo, 1)
            for i in range(G * J):
                pool.wait_ge(hid_done, i + 1)
                pool.wait_ge(hid_hi, i + 1)
                if i >= 3:
                    pool.wait_ge(mm["down"], i - 2)
                nc.gpsimd.tensor_tensor(hs[1][:, i % 3, :], hid[:, i % 2, :], hs[0][:, i % 3, :],
                                        ALU.subtract).then_inc(hid_lo, 1)

        @block.scalar
        def _(act):
            def load(name, dst, src):
                act.dma_start(dst, src).then_inc(loaded[name], 16)

            load("ctx", ctx_sb[:, :], ctxT)
            load("wxq", wxq[:, 0, :], xq_wT)
            load("wxk", wxq[:, 1, :], xk_wT)
            load("xqb", xqb[:, 0:1], xq_b)
            load("xkb", xqb[:, 1:2], xk_b)
            load("consts", cst[:, :], consts)
            load("qb", qb[:, :], q_b)
            load("kb", kvb[:, 0:D], k_b.partition_broadcast(P))
            load("vb", kvb[:, D:2 * D], v_b.partition_broadcast(P))
            load("ob", ob[:, :], o_b.partition_broadcast(P))

            def copy(dst, src, done):
                nc.scalar.activation(dst, src, ACT.Copy).then_inc(done, 1)

            def split_qkv():
                for i, n in enumerate(("qw", "kw", "vw")):
                    act.wait_ge(loaded[n], 16)
                    s = slice(i * D, (i + 1) * D)
                    copy(wqkv[0][:, :, s], wqkv_raw[:, :, s], wqkv_hi)

            def cross_projection(n):
                act.wait_ge(mm["xqk"], n + 1)
                if n == 0:
                    act.wait_ge(loaded["xqb"], 16)
                    act.wait_ge(loaded["xkb"], 16)
                h, which = n // 2, n % 2
                nc.scalar.activation(xqk[:, 2 * h:2 * h + 2, which, :],
                                     bank[where["xqk", n]][:, :].rearrange("p (b s) -> p b s", b=2),
                                     ACT.Identity, bias=xqb[:, which:which + 1]).then_inc(xqk_done, 1)

            def softmax_exp(b):
                act.wait_ge(max_done, b + 1)
                for i in range(2):
                    last = nc.scalar.activation(att[:, b, i, :], bank[where["energy", b]][:, i * S:(i + 1) * S],
                                                ACT.Exp, bias=nmx[:, b, i:i + 1], accum_out=sums[:, b, i:i + 1])
                last.then_inc(exp_done, 1)

            def turn_hi(layer, n):
                act.wait_ge(mm[f"lnT{layer}"], n + 1)
                copy(lnT[0][:, n // 2, n % 2, :], bank[where[f"lnT{layer}", n]][:, :], turned_hi[layer])

            def turn_2(n):
                act.wait_ge(mm["lnT1"], n + 1)
                copy(colT[:, n // 2, n % 2, :], bank[where["lnT1", n]][:, :], turned2)

            def turn_attn(n):
                act.wait_ge(mm["aT"], n + 1)
                copy(colT[:, n // 2, n % 2, :], bank[where["aT", n]][:, :], aT_done)

            def turn_att(b):
                act.wait_ge(mm["attT"], b + 1)
                copy(attT[:, b, :, :].rearrange("p k s -> p (k s)"), bank[where["attT", b]][:, :], attT_done)

            def q_parts(n):
                act.wait_ge(mm["q"], n + 1)
                if n == 0:
                    act.wait_ge(loaded["qb"], 16)
                    act.wait_ge(ready, 1)
                if n >= 2:
                    act.wait_ge(q_done, n - 1)
                g, m = n // 2, n % 2
                src = bank[where["q", n]][:, :]
                nc.scalar.activation(eq[:, m, :], src, ACT.Relu, scale=-1.0, bias=qbn[:, m:m + 1]).then_inc(q_clamped, 1)
                nc.scalar.activation(qp[:, g, m, :], src, ACT.Identity, bias=qb1[:, m:m + 1])
                act.wait_ge(q_clamped, n + 1)
                nc.scalar.activation(eq[:, m, :], eq[:, m, :], ACT.Exp, scale=-1.0).then_inc(q_exp, 1)

            def k_part(t):
                act.wait_ge(kv_done, t + 1)
                if t >= TG:
                    act.wait_ge(k_done, t - TG + 1)
                e = ek[:, t % TG, :]
                nc.scalar.activation(e.rearrange("p (k c) -> p k c", k=K), kvs[:, t, 0:K, 0:P],
                                     ACT.Relu, scale=-1.0, bias=one[:, 0:1]).then_inc(k_clamped, 1)
                act.wait_ge(k_clamped, t + 1)
                nc.scalar.activation(e, e, ACT.Exp, scale=-1.0).then_inc(k_exp, 1)

            def split_w13(m):
                act.wait_ge(loaded[("w10", "w11", "w30", "w31")[m]], 16)
                copy(w13[0][:, m // 2, m % 2, :], w13_raw[:, m % 2, :], w13_hi)

            def split_w2(n):
                act.wait_ge(fly, 6)
                if n:
                    act.wait_ge(mm["w2h"], n)
                    act.wait_ge(w2s_lo, n)
                copy(w2s[0][:, :, :], w2b[:, 2 * n:2 * n + 2, :], w2s_hi)

            def turned_w2(n):
                act.wait_ge(mm["w2h"], n + 1)
                nc.scalar.activation(w2[0][:, 2 * n:2 * n + 2, :].rearrange("p j d -> p (j d)"),
                                     bank[where["w2h", n]][:, :], ACT.Copy, scale=HAD_SCALE).then_inc(w2_hi, 1)

            def silu(i):
                act.wait_ge(mm["gate"], i + 1)
                if i >= 2:
                    act.wait_ge(hid_done, i - 1)
                nc.scalar.activation(gated[:, i % 2, :], bank[where["gate", i]][:, :], ACT.Silu).then_inc(silu_done, 1)

            def hidden_hi(i):
                act.wait_ge(hid_done, i + 1)
                if i >= 3:
                    act.wait_ge(mm["down"], i - 2)
                copy(hs[0][:, i % 3, :], hid[:, i % 2, :], hid_hi)

            act.wait_ge(ready, 1)
            split_qkv()
            for n in range(4):
                cross_projection(n)
            turn_hi(0, 0)
            turn_hi(0, 1)
            softmax_exp(0)
            softmax_exp(1)
            q_parts(0)
            q_parts(1)
            for t in range(TG):
                k_part(t)
            turn_hi(0, 2)
            turn_hi(0, 3)
            softmax_exp(2)
            softmax_exp(3)
            turn_att(0)
            turn_att(1)
            q_parts(2)
            q_parts(3)
            split_w13(0)
            split_w13(1)
            for t in range(TG, T):
                k_part(t)
            turn_attn(0)
            turn_attn(1)
            turn_att(2)
            turn_att(3)
            split_w2(0)
            turn_2(0)
            turn_2(1)
            turned_w2(0)
            split_w2(1)
            turned_w2(1)
            split_w2(2)
            turn_attn(2)
            turn_attn(3)
            split_w13(2)
            split_w13(3)
            turned_w2(2)
            split_w2(3)
            turned_w2(3)
            turn_hi(2, 0)
            turn_hi(2, 1)
            for i in range(G * J):
                silu(i)
                hidden_hi(i)
                if i == 1:
                    turn_2(2)
                    turn_2(3)
                if i == 5:
                    turn_hi(2, 2)
                    turn_hi(2, 3)

        @block.vector
        def _(dve):
            links = [0]

            def link(ins):
                links[0] += 1
                ins.then_inc(chain, 1)

            def settle():
                dve.wait_ge(chain, links[0])

            def layernorm(layer, g):
                t0 = g * TG
                for t in range(TG):
                    if layer == 0 and t == 0:
                        dve.wait_ge(loaded[f"x{g}"], 16)
                    if layer == 1 and t % 2 == 0:
                        dve.wait_ge(x1_done, 2 * g + t // 2 + 1)
                    if layer == 2 and t % 2 == 0:
                        dve.wait_ge(x2_done, 2 * g + t // 2 + 1)
                    link(nc.vector.bn_stats(stats[:, t, :], res[:, t0 + t, :]))
                settle()
                for t in range(TG):
                    link(nc.vector.bn_aggr(mv[:, t, :], stats[:, t, :]))
                settle()
                link(nc.vector.tensor_scalar(ve[:, :], mv[:, :, 1], LN_EPS, None, ALU.add))
                settle()
                link(nc.vector.tensor_scalar(nt[:, :].bitcast(i32), ve[:, :].bitcast(i32), 1, None,
                                             ALU.logical_shift_right))
                settle()
                link(nc.vector.tensor_scalar(rstd[:, :].bitcast(i32), nt[:, :].bitcast(i32), -1, RSQRT_SEED,
                                             ALU.mult, ALU.add))
                settle()
                for _ in range(3):
                    link(nc.vector.tensor_tensor(nt[:, :], rstd[:, :], rstd[:, :], ALU.mult))
                    settle()
                    link(nc.vector.scalar_tensor_tensor(out=nt[:, :], in0=nt[:, :], scalar=-0.5, in1=ve[:, :],
                                                        op0=ALU.mult, op1=ALU.mult))
                    settle()
                    link(nc.vector.scalar_tensor_tensor(out=rstd[:, :], in0=nt[:, :], scalar=1.5, in1=rstd[:, :],
                                                        op0=ALU.add, op1=ALU.mult))
                    settle()
                for t in range(TG):
                    nc.vector.tensor_scalar(ln[:, t0 + t, :], res[:, t0 + t, :], mv[:, t, 0:1], rstd[:, t:t + 1],
                                            ALU.subtract, ALU.mult).then_inc(normed[layer], 1)

            def turn_lo(layer, n):
                dve.wait_ge(turned_hi[layer], n + 1)
                dve.wait_ge(mm[f"lnT{layer}"], n + 1)
                nc.vector.tensor_tensor(lnT[1][:, n // 2, n % 2, :], bank[where[f"lnT{layer}", n]][:, :],
                                        lnT[0][:, n // 2, n % 2, :].bitcast(f32),
                                        ALU.subtract).then_inc(turned_lo[layer], 1)

            def row_max(b):
                dve.wait_ge(mm["energy"], b + 1)
                nc.vector.reduce_max(nmx[:, b, :], bank[where["energy", b]][:, :].rearrange("p (i s) -> p i s", i=2),
                                     AX.X, negate=True).then_inc(max_done, 1)

            def softmax_norm(b):
                dve.wait_ge(exp_done, b + 1)
                link(nc.vector.reciprocal(rsum[:, b, :], sums[:, b, :]))
                settle()
                for i in range(2):
                    last = nc.vector.tensor_scalar(att[:, b, i, :], att[:, b, i, :], rsum[:, b, i:i + 1], None, ALU.mult)
                last.then_inc(att_done, 1)

            def q_elu(n):
                dve.wait_ge(q_exp, n + 1)
                g, m = n // 2, n % 2
                nc.vector.tensor_tensor(qp[:, g, m, :], eq[:, m, :], qp[:, g, m, :], ALU.max).then_inc(q_done, 1)

            def kv_bias(t):
                dve.wait_ge(mm["kv"], t + 1)
                nc.vector.tensor_tensor(kvs[:, t, :, 0:P], bank[where["kv", t]][:, :].rearrange("p (c w) -> p c w", w=P),
                                        kvb[:, :].rearrange("p (c w) -> p c w", w=P), ALU.add).then_inc(kv_done, 1)

            def k_elu(t):
                dve.wait_ge(k_exp, t + 1)
                k1 = kvs[:, t, 0:K, 0:P]
                nc.vector.tensor_tensor(k1, ek[:, t % TG, :].rearrange("p (k c) -> p k c", k=K), k1,
                                        ALU.max).then_inc(k_done, 1)

            def kv_blocks(b):
                dve.wait_ge(mm["kvm"], b + 1)
                src = bank[where["kvm", b]][:, 0:K * KVW].rearrange("p (k w) -> p k w", k=K)
                nc.vector.tensor_tensor(kvx[:, b, :, 0:P], src[:, :, 0:P],
                                        headmask.unsqueeze(1).to_broadcast([P, K, P]), ALU.mult)
                nc.vector.tensor_tensor(kvx[:, b, :, P:P + HC], src[:, :, P:P + 1].to_broadcast([P, K, HC]),
                                        headcols.unsqueeze(1).to_broadcast([P, K, HC]), ALU.mult).then_inc(kvx_done, 1)

            def attn_rows(t):
                dve.wait_ge(mm["attn"], t + 1)
                src = bank[where["attn", t]][:, 0:K * (P + HC)].rearrange("p (k w) -> p k w", k=K)
                link(nc.vector.tensor_scalar(zs[:, :, :], src[:, :, P:P + HC], Z_EPS, None, ALU.add))
                settle()
                link(nc.vector.reciprocal(rz[:, :, :], zs[:, :, :]))
                settle()
                nc.vector.tensor_tensor(ln[:, t, :].rearrange("p (k h e) -> p k h e", k=K, h=HC),
                                        src[:, :, 0:P].rearrange("p k (h e) -> p k h e", h=HC),
                                        rz[:, :, :].unsqueeze(3).to_broadcast([P, K, HC, HD]),
                                        ALU.mult).then_inc(attn_done, 1)

            def add_residual(kind, n, done):
                dve.wait_ge(mm[kind], n + 1)
                two = res[:, 2 * n:2 * n + 2, :].rearrange("p t c -> p (t c)")
                nc.vector.tensor_tensor(two, bank[where[kind, n]][:, :], two, ALU.add).then_inc(done, 1)

            def w2_low(n):
                dve.wait_ge(w2_hi, n + 1)
                dve.wait_ge(mm["w2h"], n + 1)
                nc.vector.scalar_tensor_tensor(out=w2[1][:, 2 * n:2 * n + 2, :].rearrange("p j d -> p (j d)"),
                                               in0=bank[where["w2h", n]][:, :], scalar=HAD_SCALE,
                                               in1=w2[0][:, 2 * n:2 * n + 2, :].rearrange("p j d -> p (j d)").bitcast(f32),
                                               op0=ALU.mult, op1=ALU.subtract).then_inc(w2_lo, 1)

            def hidden(i):
                dve.wait_ge(silu_done, i + 1)
                dve.wait_ge(mm["lin"], i + 1)
                if i >= 2:
                    dve.wait_ge(hid_hi, i - 1)
                    dve.wait_ge(hid_lo, i - 1)
                nc.vector.tensor_tensor(hid[:, i % 2, :], bank[where["lin", i]][:, :], gated[:, i % 2, :],
                                        ALU.mult).then_inc(hid_done, 1)

            def output(n):
                dve.wait_ge(mm["down"], J * (n // 2 + 1))
                two = res[:, 2 * n:2 * n + 2, :].rearrange("p t c -> p (t c)")
                nc.vector.tensor_tensor(two, bank[where["acc", n]][:, :], two, ALU.add).then_inc(out_done, 1)

            dve.wait_ge(loaded["qb"], 16)
            link(nc.vector.memset(one[:, :], 1.0))
            link(nc.vector.tensor_scalar(qbn[:, :], qb[:, :], -1.0, None, ALU.mult))
            nc.vector.tensor_scalar(qb1[:, :], qb[:, :], 1.0, None, ALU.add).then_inc(ready, 1)
            layernorm(0, 0)
            dve.wait_ge(loaded["consts"], 16)
            nc.vector.tensor_copy(had_r[:, :], had).then_inc(ready, 1)
            dve.wait_ge(loaded["kb"], 16)
            dve.wait_ge(loaded["vb"], 16)
            link(nc.vector.tensor_scalar(kvb[:, 0:D], kvb[:, 0:D], 1.0, None, ALU.add))
            settle()
            turn_lo(0, 0)
            turn_lo(0, 1)
            row_max(0)
            row_max(1)
            softmax_norm(0)
            softmax_norm(1)
            q_elu(0)
            q_elu(1)
            dve.wait_ge(wqkv_lo, 3)
            link(nc.vector.memset(kvs[:, :, K:2 * K, P:P + 1], 1.0))
            for t in range(TG):
                kv_bias(t)
                if t:
                    k_elu(t - 1)
            k_elu(TG - 1)
            layernorm(0, 1)
            turn_lo(0, 2)
            turn_lo(0, 3)
            row_max(2)
            row_max(3)
            kv_blocks(0)
            kv_blocks(1)
            softmax_norm(2)
            softmax_norm(3)
            q_elu(2)
            q_elu(3)
            for t in range(TG):
                attn_rows(t)
            for t in range(TG, T):
                kv_bias(t)
                if t > TG:
                    k_elu(t - 1)
            k_elu(T - 1)
            dve.wait_ge(xob_done, 1)
            add_residual("o", 0, x1_done)
            add_residual("o", 1, x1_done)
            layernorm(1, 0)
            kv_blocks(2)
            kv_blocks(3)
            for t in range(TG, T):
                attn_rows(t)
            w2_low(0)
            w2_low(1)
            add_residual("xm", 0, x2_done)
            add_residual("xm", 1, x2_done)
            layernorm(2, 0)
            dve.wait_ge(xob_done, 2)
            add_residual("o", 2, x1_done)
            add_residual("o", 3, x1_done)
            w2_low(2)
            w2_low(3)
            turn_lo(2, 0)
            turn_lo(2, 1)
            layernorm(1, 1)
            for i in range(G * J):
                hidden(i)
                if i == 2:
                    add_residual("xm", 2, x2_done)
                    add_residual("xm", 3, x2_done)
                if i == 3:
                    layernorm(2, 1)
                if i == 5:
                    turn_lo(2, 2)
                    turn_lo(2, 3)
                if i == J + 1:
                    output(0)
                    output(1)
            output(2)
            output(3)

        @block.tensor
        def _(pe):
            def claim(*unit):
                if before[unit] is not None:
                    pe.wait_ge(*emptied(before[unit]))
                return bank[where[unit]]

            def cross_projection(n):
                h, which = n // 2, n % 2
                ps = claim("xqk", n)
                if n == 0:
                    pe.wait_ge(loaded["ctx"], 16)
                    pe.wait_ge(loaded["wxq"], 16)
                if n == 1:
                    pe.wait_ge(loaded["wxk"], 16)
                nc.tensor.matmul(ps[:, :], wxq[:, which, :], ctx_sb[:, h * N:(h + 1) * N],
                                 start=True, stop=True).then_inc(mm["xqk"], 1)

            def energy(b):
                ps = claim("energy", b)
                pe.wait_ge(xqk_done, 2 * (b // 2) + 2)
                for i in range(2):
                    last = nc.tensor.matmul(ps[:, i * S:(i + 1) * S], xqk[:, b, 0, i * P:(i + 1) * P], xqk[:, b, 1, :],
                                            start=True, stop=True)
                last.then_inc(mm["energy"], 1)

            def turn_rows(stage, g, rows_done):
                pair = [claim(stage, 2 * g + c) for c in range(K)]
                if stage == "lnT0" and g == 0:
                    pe.wait_ge(loaded["consts"], 16)
                for t in range(TG):
                    pe.wait_ge(rows_done, g * TG + t + 1)
                    for c in range(K):
                        last = nc.tensor.transpose(pair[c][:, t * P:(t + 1) * P],
                                                   ln[:, g * TG + t, c * P:(c + 1) * P], ident)
                        if t == TG - 1:
                            last.then_inc(mm[stage], 1)

            def turn_att(b):
                ps = claim("attT", b)
                pe.wait_ge(att_done, b + 1)
                for k in range(K):
                    for i in range(2):
                        last = nc.tensor.transpose(ps[:, k * S + i * P:k * S + (i + 1) * P],
                                                   att[:, b, i, k * P:(k + 1) * P], ident)
                last.then_inc(mm["attT"], 1)

            def query(n):
                g, m = n // 2, n % 2
                ps = claim("q", n)
                pe.wait_ge(turned_hi[0], 2 * g + 2)
                pe.wait_ge(turned_lo[0], 2 * g + 2)
                pe.wait_ge(wqkv_lo, 1)
                for i, (wp, xp) in enumerate(PARTS):
                    for k in range(K):
                        last = nc.tensor.matmul(ps[:, :], wqkv[wp][:, k, m * P:(m + 1) * P], lnT[xp][:, g, k, :],
                                                start=(i == 0 and k == 0), stop=(i == 2 and k == K - 1))
                last.then_inc(mm["q"], 1)

            def key_value(t):
                g, r = t // TG, t % TG
                ps = claim("kv", t)
                pe.wait_ge(wqkv_lo, 3)
                for i, (wp, xp) in enumerate(PARTS):
                    for k in range(K):
                        last = nc.tensor.matmul(ps[:, :], lnT[xp][:, g, k, r * P:(r + 1) * P], wqkv[wp][:, k, D:3 * D],
                                                start=(i == 0 and k == 0), stop=(i == 2 and k == K - 1))
                last.then_inc(mm["kv"], 1)

            def key_times_value(b):
                ps = claim("kvm", b)
                pe.wait_ge(k_done, 2 * b + 2)
                for c in range(K):
                    for i in range(2):
                        last = nc.tensor.matmul(ps[:, c * KVW:(c + 1) * KVW], kvs[:, 2 * b + i, c, 0:P],
                                                kvs[:, 2 * b + i, K + c, :], start=(i == 0), stop=(i == 1))
                last.then_inc(mm["kvm"], 1)

            def attention(t):
                g, r = t // TG, t % TG
                ps = claim("attn", t)
                pe.wait_ge(q_done, 2 * g + 2)
                pe.wait_ge(kvx_done, t // 2 + 1)
                W = P + HC
                for c in range(K):
                    last = nc.tensor.matmul(ps[:, c * W:(c + 1) * W], qp[:, g, c, r * P:(r + 1) * P],
                                            kvx[:, t // 2, c, :], start=True, stop=True)
                last.then_inc(mm["attn"], 1)

            def rows_times(stage, n, weights):
                ps = claim(stage, n)
                for i in range(2):
                    t = 2 * (n % 2) + i
                    for k in range(K):
                        last = nc.tensor.matmul(ps[:, i * D:(i + 1) * D], colT[:, n // 2, k, t * P:(t + 1) * P],
                                                weights(k), start=(k == 0), stop=(k == K - 1))
                last.then_inc(mm[stage], 1)

            def project(g):
                pe.wait_ge(aT_done, 2 * g + 2)
                pe.wait_ge(loaded["ow"], 16)
                for n in (2 * g, 2 * g + 1):
                    rows_times("o", n, lambda k: wo[:, k, :])

            def cross(g):
                pe.wait_ge(turned2, 2 * g + 2)
                pe.wait_ge(attT_done, 2 * g + 2)
                for n in (2 * g, 2 * g + 1):
                    rows_times("xm", n, lambda k: attT[:, n, k, :])

            def hadamard(n):
                ps = claim("w2h", n)
                pe.wait_ge(ready, 2)
                pe.wait_ge(w2s_hi, n + 1)
                pe.wait_ge(w2s_lo, n + 1)
                for part in (1, 0):
                    last = nc.tensor.matmul(ps[:, :], had_r[:, :], w2s[part][:, :, :].rearrange("p j d -> p (j d)"),
                                            start=(part == 1), stop=(part == 0))
                last.then_inc(mm["w2h"], 1)

            def up(i):
                g, j = i // J, i % J
                if j == 0:
                    pe.wait_ge(turned_hi[2], 2 * g + 2)
                    pe.wait_ge(turned_lo[2], 2 * g + 2)
                if i == 0:
                    pe.wait_ge(w13_hi, 4)
                    pe.wait_ge(w13_lo, 4)
                for which, stage in enumerate(("gate", "lin")):
                    ps = claim(stage, i)
                    for n, (wp, xp) in enumerate(PARTS):
                        for k in range(K):
                            last = nc.tensor.matmul(ps[:, :], w13[wp][:, which, k, j * P:(j + 1) * P],
                                                    lnT[xp][:, g, k, :], start=(n == 0 and k == 0),
                                                    stop=(n == 2 and k == K - 1))
                    last.then_inc(mm[stage], 1)

            def down(i):
                g, j = i // J, i % J
                if j == 0:
                    for n in range(2):
                        claim("acc", 2 * g + n)
                if i == 0:
                    pe.wait_ge(w2_lo, 4)
                pe.wait_ge(hid_hi, i + 1)
                pe.wait_ge(hid_lo, i + 1)
                for t in range(TG):
                    ps = bank[ACC[t // 2]][:, (t % 2) * D:(t % 2 + 1) * D]
                    for n, (wp, xp) in enumerate(PARTS):
                        last = nc.tensor.matmul(ps, hs[xp][:, i % 3, t * P:(t + 1) * P], w2[wp][:, j, :],
                                                start=(j == 0 and n == 0 and t % 2 == 0),
                                                stop=(j == J - 1 and n == 2 and t % 2 == 1), skip_group_check=True)
                last.then_inc(mm["down"], 1)

            for n in range(4):
                cross_projection(n)
            turn_rows("lnT0", 0, normed[0])
            energy(0)
            energy(1)
            query(0)
            query(1)
            for t in range(TG):
                key_value(t)
            energy(2)
            energy(3)
            turn_rows("lnT0", 1, normed[0])
            turn_att(0)
            turn_att(1)
            key_times_value(0)
            key_times_value(1)
            query(2)
            query(3)
            for t in range(TG):
                attention(t)
            for t in range(TG, T):
                key_value(t)
            turn_rows("aT", 0, attn_done)
            turn_att(2)
            turn_att(3)
            project(0)
            key_times_value(2)
            key_times_value(3)
            for t in range(TG, T):
                attention(t)
            turn_rows("lnT1", 0, normed[1])
            hadamard(0)
            hadamard(1)
            turn_rows("aT", 1, attn_done)
            cross(0)
            project(1)
            hadamard(2)
            hadamard(3)
            turn_rows("lnT2", 0, normed[2])
            for i in range(G * J):
                up(i)
                if i == 1:
                    turn_rows("lnT1", 1, normed[1])
                if i == 2:
                    cross(1)
                if i == 5:
                    turn_rows("lnT2", 1, normed[2])
                if i >= 2:
                    down(i - 2)
            down(G * J - 2)
            down(G * J - 1)


def kernel(**inputs):
    import numpy as np
    import concourse.bacc as bacc
    from concourse.bass_utils import run_bass_kernel_spmd

    P, HD, D = 128, 16, 256
    ones = np.ones((1, 1), np.float32)
    had = ones
    while had.shape[0] < P:
        had = np.block([[had, had], [had, -had]])
    heads = np.arange(P) // HD
    consts = np.concatenate([
        np.eye(P, dtype=np.float32), had.astype(np.float32),
        (heads[:, None] == heads[None, :]).astype(np.float32),
        (heads[:, None] == np.arange(P // HD)[None, :]).astype(np.float32)], axis=1)

    a = {n: np.asarray(v) for n, v in inputs.items()}
    arrays = {
        "x": a["x"].reshape(-1, D),
        "ctxT": a["ctx_1024"].reshape(-1, P).T,
        "q_wT": a["L0_attn_q_w"].T, "k_wT": a["L0_attn_k_w"].T, "v_wT": a["L0_attn_v_w"].T, "o_wT": a["L0_attn_o_w"].T,
        "xq_wT": a["L0_xattn_Wq"].T, "xk_wT": a["L0_xattn_Wk"].T,
        "w1T": a["L0_ffn_W1"].T, "w3T": a["L0_ffn_W3"].T, "w2T": a["L0_ffn_W2"].T,
        "q_b": a["L0_attn_q_b"].reshape(-1, P).T,
        "xq_b": a["L0_xattn_bq"].reshape(P, 1), "xk_b": a["L0_xattn_bk"].reshape(P, 1),
        "k_b": a["L0_attn_k_b"], "v_b": a["L0_attn_v_b"], "o_b": a["L0_attn_o_b"],
        "consts": consts,
    }
    arrays = {n: np.ascontiguousarray(v) for n, v in arrays.items()}
    nc = bacc.Bacc("TRN2", target_bir_lowering=False, num_devices=1)
    aps = [nc.dram_tensor(n, v.shape, mybir.dt.float32, kind="ExternalInput").ap() for n, v in arrays.items()]
    out = nc.dram_tensor("out", (a["x"].size // D, D), mybir.dt.float32, kind="ExternalOutput").ap()
    decoder_layer(nc, *aps, out)
    r = run_bass_kernel_spmd(nc, [arrays], core_ids=[0])
    return r.results[0]["out"].reshape(a["x"].shape)
```

```python
import concourse.bass as bass
from concourse import mybir
from contextlib import ExitStack


def decoder_layer(nc, x, ctxT, q_wT, kv_wT, o_wT, xqk_wT, w1T, w3T, w2T, row_bias, cols, out):
    f32, f32r, i32 = mybir.dt.float32, mybir.dt.float32r, mybir.dt.int32
    ALU, ACT, AX = mybir.AluOpType, mybir.ActivationFunctionType, mybir.AxisListType

    P = 128
    TOK, D = x.shape
    T = TOK // P
    B = 4
    S = TOK // B
    G, TG = 2, T // 2
    N = TG * P
    K = D // P
    HD = 16
    HC = P // HD
    H = w1T.shape[1]
    J = H // P
    LN_EPS, Z_EPS = 1e-5, 1e-6
    RSQRT_SEED = 0x5F3759DF
    HAD_SCALE = 1.0 / float(H) ** 0.5
    PARTS = ((1, 0), (0, 1), (0, 0))

    tiles = lambda ap: ap.rearrange("(t p) c -> p t c", p=P)

    ctx = ExitStack()
    with ctx:
        def sb(name, shape, dt=f32):
            return ctx.enter_context(nc.sbuf_tensor(name, shape, dt))

        def sem(name):
            return ctx.enter_context(nc.semaphore(name))

        res = sb("res", [P, T, D])
        ln = sb("ln", [P, T, D])
        lnT = [sb("lnT_hi", [P, G, K, N], f32r), sb("lnT_lo", [P, G, K, N], f32r)]
        colT = sb("colT", [P, G, K, N])
        qp = sb("qp", [P, G, K, N])
        eq = sb("eq", [P, K, N])
        KVW = P + 1
        kvs = sb("kvs", [P, T, 2 * K, KVW])
        ctx_sb = sb("ctx_sb", [P, TOK])
        ek = ctx_sb[:, :].rearrange("p (t c) -> p t c", c=D)
        wqkv = [sb("wqkv_hi", [P, K, 3 * D], f32r), sb("wqkv_lo", [P, K, 3 * D], f32r)]
        wqkv_raw = kvs[:, :, :, :].rearrange("p t c w -> p (t c w)")[:, 0:K * 3 * D].rearrange(
            "p (k n) -> p k n", k=K)
        wo = sb("wo", [P, K, D])
        wxq = sb("wxq", [P, 2, P])
        xqk = sb("xqk", [P, B, 2, S])
        att = xqk
        attT = sb("attT", [P, B, K, S])
        w13_raw = sb("w13_raw", [P, 2, H])
        w13 = [sb("w13_hi", [P, 2, K, H], f32r), sb("w13_lo", [P, 2, K, H], f32r)]
        w2a = sb("w2a", [P, J, D])
        w2b = sb("w2b", [P, J, D])
        w2s = [sb("w2s_hi", [P, 2, 2, D], f32r), sb("w2s_lo", [P, 2, 2, D], f32r)]
        w2 = [sb("w2_hi", [P, J, D], f32r), sb("w2_lo", [P, J, D], f32r)]
        kvx = sb("kvx", [P, B, K, P + HC])
        gated = qp[:, 0, :, :]
        hid = eq
        hs = [sb("hid_hi", [P, 3, N], f32r), sb("hid_lo", [P, 3, N], f32r)]
        rowb = sb("rowb", [P, 3 * D])
        kvb, ob = rowb[:, 0:2 * D], rowb[:, 2 * D:3 * D]
        qb1 = sb("qb1", [P, K])
        cst = sb("cst", [P, 3 * P + HC + K + 2])
        ident, had, headmask = cst[:, 0:P], cst[:, P:2 * P], cst[:, 2 * P:3 * P]
        headcols = cst[:, 3 * P:3 * P + HC]
        qb, xqb = cst[:, 3 * P + HC:3 * P + HC + K], cst[:, 3 * P + HC + K:3 * P + HC + K + 2]
        had_r = sb("had_r", [P, P], f32r)
        stats = sb("stats", [P, 3, T, 6])
        mv = sb("mv", [P, 3, T, 2])
        ve = sb("ve", [P, 3, T])
        nt = sb("nt", [P, 3, T])
        neg1 = sb("neg1", [P, 1])
        rstd = sb("rstd", [P, 3, T])
        shift2 = sb("shift2", [P, T])
        nqb = sb("nqb", [P, K])
        sh = sb("sh", [P, 3, T])
        nmx = sb("nmx", [P, B, 2])
        sums = sb("sums", [P, B, 2])
        rsum = sb("rsum", [P, B, 2])
        zs = sb("zs", [P, T, K, HC])
        rz = sb("rz", [P, T, K, HC])

        bank = [ctx.enter_context(nc.psum_tensor(f"bank{i}", [P, 512], f32)) for i in range(8)]
        ACC = (6, 7)
        NEGATED = (0, 1)
        LAST = 2
        where = {}
        before = {}
        last_in = [None] * 8

        def place(unit, b):
            where[unit], before[unit], last_in[b] = b, last_in[b], unit

        DMA_NAMES = ("x0a", "x0b", "x1", "cols", "ctx0", "ctx1", "wxqk", "qw", "kvw", "w2", "ow", "w10", "w11", "w30", "w31", "rowb")
        loaded = {n: sem("loaded_" + n) for n in DMA_NAMES}
        mm = {n: sem("mm_" + n) for n in ("xqk", "lnT0", "lnT1", "lnT2", "energy", "q", "kv", "kvm", "attn",
                                          "aT", "attT", "o", "xm", "w2h", "gate", "lin", "down", "acc")}
        chain = sem("dve_chain")
        normed = {(0, 0): sem("ln1_rows0"), (0, 1): sem("ln1_rows1"), (2, 0): sem("ln3_rows0"), (2, 1): sem("ln3_rows1")}
        scaled = {k: sem("scaled%d%d" % k) for k in normed}
        rsum_done = sem("rsum_done")
        scale2 = sem("ln2_scale")
        shifted2 = sem("ln2_shifted")
        turned_hi = {0: sem("ln1T_hi"), 2: sem("ln3T_hi")}
        turned_lo = {0: sem("ln1T_lo"), 2: sem("ln3T_lo")}
        turned2 = sem("ln2T")
        xqk_done = sem("xqk_done")
        max_done = sem("max_done")
        exp_done = sem("exp_done")
        att_done = [sem(f"att_done{i}") for i in range(4)]
        attT_done = sem("attT_done")
        q_min = [sem(f"q_min{i}") for i in range(4)]
        k_min = sem("k_min")
        q_exp = sem("q_exp")
        q_done = sem("q_done")
        kv_done = sem("kv_done")
        k_exp = sem("k_exp")
        k_done = sem("k_done")
        kvx_done = sem("kvx_done")
        attn_done = sem("attn_done")
        aT_done = sem("aT_done")
        xob_done = sem("xob_done")
        x1_done = sem("x1_done")
        x2_done = sem("x2_done")
        ready = sem("ready")
        wqkv_hi = sem("wqkv_hi_done")
        wqkv_lo = sem("wqkv_lo_done")
        w13_hi = sem("w13_hi_done")
        w13_lo = sem("w13_lo_done")
        fly = sem("w2_butterfly")
        w2s_hi = sem("w2s_hi_done")
        w2s_lo = sem("w2s_lo_done")
        w2_hi = sem("w2_hi_done")
        w2_lo = sem("w2_lo_done")
        silu_done = sem("silu_done")
        hid_done = sem("hid_done")
        hid_hi = sem("hid_hi_done")
        hid_lo_last = sem("hid_lo_last_done")
        hid_lo = sem("hid_lo_done")
        out_done = sem("out_done")
        stored = sem("stored")

        def emptied(unit):
            kind, n = unit
            return {"xqk": xqk_done, "lnT0": turned_lo[0], "lnT1": turned2, "lnT2": turned_lo[2],
                    "energy": exp_done, "q": q_done, "kv": kv_done, "kvm": kvx_done, "attn": attn_done,
                    "aT": aT_done, "attT": attT_done, "o": x1_done, "xm": x2_done, "w2h": w2_lo,
                    "gate": silu_done, "lin": hid_done, "acc": out_done}[kind], 2 * n + 2 if kind in ("xm", "acc") else n + 1

        BANKS = (
            (("xqk", 0), ("energy", 2), ("kv", 2), ("kv", 4), ("o", 1), ("attT", 1), ("attn", 6), ("o", 2),),
            (("xqk", 1), ("energy", 3), ("kv", 3), ("aT", 0), ("w2h", 0), ("w2h", 2), ("attn", 7), ("o", 3),),
            (("xqk", 2), ("q", 0), ("kvm", 0), ("aT", 1), ("attT", 0), ("xm", 0), ("aT", 2), ("lnT1", 2),),
            (("energy", 0), ("q", 1), ("kvm", 1), ("q", 2), ("kv", 7), ("xm", 1), ("aT", 3), ("lnT1", 3), ("xm", 2),
             ("lnT2", 3),),
            (("energy", 1), ("kv", 0), ("attn", 0), ("kv", 5), ("kvm", 2), ("attn", 4), ("attT", 3), ("xm", 3),),
            (("xqk", 3), ("lnT0", 2), ("attn", 1), ("q", 3), ("lnT1", 0), ("kvm", 3), ("w2h", 3), ("lnT2", 2),),
            (("lnT0", 0), ("lnT0", 3), ("attn", 2), ("kv", 6), ("lnT1", 1), ("attT", 2), ("lnT2", 0),),
            (("lnT0", 1), ("kv", 1), ("attn", 3), ("o", 0), ("w2h", 1), ("attn", 5), ("lnT2", 1),),
        )
        for b, units in enumerate(BANKS):
            for unit in units:
                place(unit, b)
        for i in range(G * J):
            place(("gate", i), (2 * i) % 3)
            place(("lin", i), (2 * i + 1) % 3)
        for n in range(2 * G):
            place(("acc", n), ACC[n % 2])

        block = ctx.enter_context(nc.Block())

        xt = tiles(x)

        def do_load(q, nm):
            if nm in ("w10", "w11", "w30", "w31"):
                n = ("w10", "w11", "w30", "w31").index(nm)
                if n >= 2:
                    q.wait_ge(w13_lo, n - 1)
                    q.wait_ge(w13_hi, n - 1)
                w, k = (w1T, w3T)[n // 2], n % 2
                q.dma_start(w13_raw[:, n % 2, :], w[k * P:(k + 1) * P, :]).then_inc(loaded[nm], 16)
                return
            dst, src = {
                "x0a": (res[:, 0:2, :], xt[:, 0:2, :]), "x0b": (res[:, 2:TG, :], xt[:, 2:TG, :]), "x1": (res[:, TG:T, :], xt[:, TG:T, :]),
                "qw": (wqkv_raw[:, :, 0:D], q_wT.rearrange("(k p) n -> p k n", p=P)),
                "kvw": (wqkv_raw[:, :, D:3 * D], kv_wT.rearrange("(k p) n -> p k n", p=P)),
                "w2": (w2a[:, :, :], w2T.rearrange("(j p) d -> p j d", p=P)),
                "ow": (wo[:, :, :], o_wT.rearrange("(k p) n -> p k n", p=P)),
                "wxqk": (wxq[:, :, :], xqk_wT.rearrange("c (w d) -> c w d", w=2)),
                "ctx0": (ctx_sb[:, 0:N], ctxT[:, 0:N]), "ctx1": (ctx_sb[:, N:TOK], ctxT[:, N:TOK]),
                "cols": (cst[:, :], cols), "rowb": (rowb[:, :], row_bias.partition_broadcast(P))}[nm]
            q.dma_start(dst, src).then_inc(loaded[nm], 16)

        @block.sync
        def _(sp):
            for nm in ("wxqk", "x0a", "x0b", "ctx1", "qw", "w10", "w11", "w2", "w30", "w31"):
                do_load(sp, nm)
            ot = tiles(out)
            for n in range(2 * G - 1):
                sp.wait_ge(out_done, 2 * n + 2)
                sp.dma_start(ot[:, 2 * n:2 * n + 2, :], res[:, 2 * n:2 * n + 2, :]).then_inc(stored, 16)
            for t in (T - 2, T - 1):
                sp.wait_ge(out_done, t + 1)
                sp.dma_start(ot[:, t:t + 1, :], res[:, t:t + 1, :]).then_inc(stored, 16)
            sp.wait_ge(stored, (2 * G + 1) * 16)

        @block.gpsimd
        def _(pool):
            def split_qkv(i):
                n, s = (("qw", slice(0, D)), ("kvw", slice(D, 3 * D)))[i]
                pool.wait_ge(loaded[n], 16)
                pool.wait_ge(wqkv_hi, i + 1)
                nc.gpsimd.tensor_tensor(wqkv[1][:, :, s], wqkv_raw[:, :, s], wqkv[0][:, :, s],
                                        ALU.subtract).then_inc(wqkv_lo, 1)

            def residual_bias(g):
                pool.wait_ge(loaded["rowb"], 16)
                pool.wait_ge(normed[0, g], TG)
                half = res[:, g * TG:(g + 1) * TG, :]
                nc.gpsimd.tensor_tensor(half, half, ob[:, :].unsqueeze(1).to_broadcast([P, TG, D]),
                                        ALU.add).then_inc(xob_done, 1)

            def butterfly(n):
                s, which = n // 2, n % 2
                step = (1, 2, 4)[s]
                src, dst = ((w2a, w2b), (w2b, w2a))[s % 2]
                if n == 0:
                    pool.wait_ge(loaded["w2"], 16)
                if s and which == 0:
                    pool.wait_ge(fly, 2 * s)
                a = src[:, :, :].rearrange("p (u two v) d -> p u two (v d)", two=2, v=step)
                o = dst[:, :, :].rearrange("p (u two v) d -> p u two (v d)", two=2, v=step)
                nc.gpsimd.tensor_tensor(o[:, :, which, :], a[:, :, 0, :], a[:, :, 1, :], (ALU.add, ALU.subtract)[which]).then_inc(fly, 1)

            def split_w13(m):
                pool.wait_ge(loaded[("w10", "w11", "w30", "w31")[m]], 16)
                pool.wait_ge(w13_hi, m + 1)
                nc.gpsimd.tensor_tensor(w13[1][:, m // 2, m % 2, :], w13_raw[:, m % 2, :],
                                        w13[0][:, m // 2, m % 2, :], ALU.subtract).then_inc(w13_lo, 1)

            def split_w2(n):
                pool.wait_ge(w2s_hi, n + 1)
                if n >= 2:
                    pool.wait_ge(mm["w2h"], n - 1)
                nc.gpsimd.tensor_tensor(w2s[1][:, n % 2, :, :], w2b[:, 2 * n:2 * n + 2, :], w2s[0][:, n % 2, :, :],
                                        ALU.subtract).then_inc(w2s_lo, 1)

            def hidden_lo(i):
                pool.wait_ge(hid_done, i + 1)
                pool.wait_ge(hid_hi, i + 1)
                if i >= 3:
                    pool.wait_ge(mm["down"], i - 2)
                nc.gpsimd.tensor_tensor(hs[1][:, i % 3, :], hid[:, i % 2, :], hs[0][:, i % 3, :],
                                        ALU.subtract).then_inc(hid_lo, 1)

            split_qkv(0)
            split_qkv(1)
            for i in range(0, 4):
                butterfly(i)
            split_w13(0)
            butterfly(4)
            butterfly(5)
            residual_bias(0)
            for i in range(0, 3):
                split_w2(i)
            split_w13(1)
            residual_bias(1)
            split_w2(3)
            split_w13(2)
            split_w13(3)
            for i in range(0, 14):
                hidden_lo(i)

        @block.scalar
        def _(act):
            for nm in ("ctx0", "cols", "x1", "ow", "kvw", "rowb"):
                do_load(act, nm)

            def copy(dst, src, done):
                nc.scalar.activation(dst, src, ACT.Copy).then_inc(done, 1)

            def split_qkv(i):
                n, part = (("qw", slice(0, D)), ("kvw", slice(D, 3 * D)))[i]
                act.wait_ge(loaded[n], 16)
                copy(wqkv[0][:, :, part], wqkv_raw[:, :, part], wqkv_hi)

            def cross_projection(n):
                act.wait_ge(mm["xqk"], n + 1)
                if n == 0:
                    act.wait_ge(loaded["cols"], 16)
                h, which = n // 2, n % 2
                nc.scalar.activation(xqk[:, 2 * h:2 * h + 2, which, :],
                                     bank[where["xqk", n]][:, :].rearrange("p (b s) -> p b s", b=2),
                                     ACT.Identity, bias=xqb[:, which:which + 1]).then_inc(xqk_done, 1)

            def softmax_exp(b):
                act.wait_ge(max_done, b + 1)
                for i in range(2):
                    last = nc.scalar.activation(att[:, b, i, :], bank[where["energy", b]][:, i * S:(i + 1) * S],
                                                ACT.Exp, bias=nmx[:, b, i:i + 1], accum_out=sums[:, b, i:i + 1])
                last.then_inc(exp_done, 1)

            def turn_hi(layer, n):
                act.wait_ge(mm[f"lnT{layer}"], n + 1)
                copy(lnT[0][:, n // 2, n % 2, :], bank[where[f"lnT{layer}", n]][:, :], turned_hi[layer])

            def turn_2(n):
                act.wait_ge(mm["lnT1"], n + 1)
                copy(colT[:, n // 2, n % 2, :], bank[where["lnT1", n]][:, :], turned2)

            def shift_row(t):
                act.wait_ge(scale2, t // TG + 1)
                nc.scalar.activation(ln[:, t, :], res[:, t, :], ACT.Identity,
                                     bias=shift2[:, t:t + 1]).then_inc(shifted2, 1)

            def turn_attn(n):
                act.wait_ge(mm["aT"], n + 1)
                copy(colT[:, n // 2, n % 2, :], bank[where["aT", n]][:, :], aT_done)

            def turn_att(b):
                act.wait_ge(mm["attT"], b + 1)
                copy(attT[:, b, :, :].rearrange("p k s -> p (k s)"), bank[where["attT", b]][:, :], attT_done)

            def q_exponential(n):
                act.wait_ge(q_min[n], 1)
                nc.scalar.activation(eq[:, n % 2, :], eq[:, n % 2, :], ACT.Exp, scale=-1.0 if n in NEGATED else 1.0).then_inc(q_exp, 1)

            def q_clamp(n):
                act.wait_ge(mm["q"], n + 1)
                act.wait_ge(ready, 1)
                if n >= 2:
                    act.wait_ge(q_done, n - 1)
                nc.scalar.activation(eq[:, n % 2, :], bank[where["q", n]][:, :], ACT.Relu, scale=-1.0,
                                     bias=nqb[:, n % 2:n % 2 + 1]).then_inc(q_min[n], 1)

            def softmax_norm(b):
                act.wait_ge(rsum_done, b + 1)
                for i in range(2):
                    last = nc.scalar.activation(att[:, b, i, :], att[:, b, i, :], ACT.Copy, scale=rsum[:, b, i:i + 1])
                last.then_inc(att_done[b], 1)

            def k_exponential(t):
                act.wait_ge(kv_done, t + 1)
                if t >= TG:
                    act.wait_ge(k_done, t - TG + 1)
                nc.scalar.activation(ek[:, t % TG, :].rearrange("p (k c) -> p k c", k=K), kvs[:, t, 0:K, 0:P], ACT.Exp,
                                     bias=neg1[:, 0:1]).then_inc(k_exp, 1)

            def split_w13(m):
                act.wait_ge(loaded[("w10", "w11", "w30", "w31")[m]], 16)
                copy(w13[0][:, m // 2, m % 2, :], w13_raw[:, m % 2, :], w13_hi)

            def split_w2(n):
                act.wait_ge(fly, 6)
                if n >= 2:
                    act.wait_ge(mm["w2h"], n - 1)
                    act.wait_ge(w2s_lo, n - 1)
                copy(w2s[0][:, n % 2, :, :], w2b[:, 2 * n:2 * n + 2, :], w2s_hi)

            def turned_w2(n):
                act.wait_ge(mm["w2h"], n + 1)
                nc.scalar.activation(w2[0][:, 2 * n:2 * n + 2, :].rearrange("p j d -> p (j d)"),
                                     bank[where["w2h", n]][:, :], ACT.Copy, scale=HAD_SCALE).then_inc(w2_hi, 1)

            def silu(i):
                act.wait_ge(mm["gate"], i + 1)
                if i >= 2:
                    act.wait_ge(hid_done, i - 1)
                nc.scalar.activation(gated[:, i % 2, :], bank[where["gate", i]][:, :], ACT.Silu).then_inc(silu_done, 1)

            def hidden_hi(i):
                act.wait_ge(hid_done, i + 1)
                if i >= 3:
                    act.wait_ge(mm["down"], i - 2)
                copy(hs[0][:, i % 3, :], hid[:, i % 2, :], hid_hi)

            for i in range(0, 3):
                cross_projection(i)
            split_qkv(0)
            cross_projection(3)
            turn_hi(0, 0)
            turn_hi(0, 1)
            split_qkv(1)
            softmax_exp(0)
            softmax_exp(1)
            q_clamp(0)
            q_exponential(0)
            q_clamp(1)
            q_exponential(1)
            softmax_exp(2)
            k_exponential(0)
            softmax_exp(3)
            k_exponential(1)
            k_exponential(2)
            turn_hi(0, 2)
            k_exponential(3)
            turn_hi(0, 3)
            split_w13(0)
            k_exponential(4)
            softmax_norm(0)
            q_exponential(2)
            split_w13(1)
            turn_attn(0)
            turn_attn(1)
            q_exponential(3)
            split_w2(0)
            split_w13(2)
            k_exponential(5)
            split_w2(1)
            turned_w2(0)
            split_w2(2)
            turn_att(0)
            k_exponential(6)
            softmax_norm(1)
            k_exponential(7)
            turn_2(0)
            turn_2(1)
            turned_w2(1)
            turn_att(1)
            turned_w2(2)
            softmax_norm(2)
            for i in range(0, 3):
                shift_row(i)
            split_w2(3)
            shift_row(3)
            turn_att(2)
            split_w13(3)
            turn_attn(2)
            turn_attn(3)
            turn_hi(2, 0)
            turn_hi(2, 1)
            turned_w2(3)
            silu(0)
            turn_2(2)
            turn_att(3)
            hidden_hi(0)
            silu(1)
            turn_2(3)
            shift_row(4)
            silu(2)
            silu(3)
            hidden_hi(1)
            shift_row(5)
            shift_row(6)
            hidden_hi(2)
            hidden_hi(3)
            silu(4)
            shift_row(7)
            for i in range(4, 7):
                hidden_hi(i)
                silu(i + 1)
            turn_hi(2, 2)
            turn_hi(2, 3)
            silu(8)
            silu(9)
            for i in range(7, 10):
                hidden_hi(i)
            silu(10)
            hidden_hi(10)
            for i in range(11, 14):
                silu(i)
            hidden_hi(11)
            hidden_hi(12)
            silu(14)
            silu(15)
            for i in range(13, 16):
                hidden_hi(i)

        @block.vector
        def _(dve):
            links = [0]
            mark = {}

            def link(ins, name):
                links[0] += 1
                mark[name] = links[0]
                ins.then_inc(chain, 1)

            def after(name):
                dve.wait_ge(chain, mark[name])

            def row_stats(layer, t):
                g = t // TG
                if layer == 0 and t in (0, 2, 4):
                    dve.wait_ge(loaded[{0: "x0a", 2: "x0b", 4: "x1"}[t]], 16)
                if layer == 1 and t % 2 == 0:
                    dve.wait_ge(x1_done, t // 2 + 1)
                if layer == 2:
                    dve.wait_ge(x2_done, t + 1)
                link(nc.vector.bn_stats(stats[:, layer, t, :], res[:, t, :]), ("bn", layer, t))

            def row_scale(layer, g, s):
                own = slice(g * TG, (g + 1) * TG)
                y, h, v = rstd[:, layer, own], nt[:, layer, own], ve[:, layer, own]
                me, pr = ("rs", layer, g, s), ("rs", layer, g, s - 1)
                if s == 0:
                    after(("bn", layer, g * TG + TG - 1))
                    for t in range(g * TG, (g + 1) * TG):
                        link(nc.vector.bn_aggr(mv[:, layer, t, :], stats[:, layer, t, :]), me)
                    return
                after(pr)
                if s == 12:
                    nc.vector.scalar_tensor_tensor(out=sh[:, layer, own], in0=mv[:, layer, own, 0], scalar=-1.0,
                                                   in1=y, op0=ALU.mult, op1=ALU.mult).then_inc(scaled[layer, g], 1)
                elif s == 1:
                    link(nc.vector.tensor_scalar(v, mv[:, layer, own, 1], LN_EPS, None, ALU.add), me)
                elif s == 2:
                    link(nc.vector.tensor_scalar(y.bitcast(i32), v.bitcast(i32), -0.5, RSQRT_SEED, ALU.mult, ALU.add), me)
                elif s % 3 == 0:
                    link(nc.vector.tensor_tensor(h, y, y, ALU.mult), me)
                elif s % 3 == 1:
                    link(nc.vector.scalar_tensor_tensor(out=h, in0=h, scalar=-0.5, in1=v, op0=ALU.mult, op1=ALU.mult), me)
                else:
                    link(nc.vector.scalar_tensor_tensor(out=y, in0=h, scalar=1.5, in1=y, op0=ALU.add, op1=ALU.mult), me)

            def normalize(layer, t):
                after(("rs", layer, t // TG, 11))
                nc.vector.tensor_scalar(ln[:, t, :], res[:, t, :], mv[:, layer, t, 0:1], rstd[:, layer, t:t + 1],
                                        ALU.subtract, ALU.mult).then_inc(normed[layer, t // TG], 1)

            def ln2_shift(g):
                after(("rs", 1, g, 11))
                own = slice(g * TG, (g + 1) * TG)
                nc.vector.scalar_tensor_tensor(out=shift2[:, own], in0=mv[:, 1, own, 0], scalar=-1.0,
                                               in1=rstd[:, 1, own], op0=ALU.mult, op1=ALU.mult).then_inc(scale2, 1)

            def add_cross(n):
                dve.wait_ge(mm["xm"], n + 1)
                for i in range(2):
                    t = 2 * n + i
                    dve.wait_ge(shifted2, t + 1)
                    nc.vector.scalar_tensor_tensor(out=res[:, t, :], in0=bank[where["xm", n]][:, i * D:(i + 1) * D],
                                                   scalar=rstd[:, 1, t:t + 1], in1=ln[:, t, :],
                                                   op0=ALU.mult, op1=ALU.add).then_inc(x2_done, 1)

            def turn_lo(layer, n):
                dve.wait_ge(turned_hi[layer], n + 1)
                dve.wait_ge(mm[f"lnT{layer}"], n + 1)
                nc.vector.tensor_tensor(lnT[1][:, n // 2, n % 2, :], bank[where[f"lnT{layer}", n]][:, :],
                                        lnT[0][:, n // 2, n % 2, :].bitcast(f32),
                                        ALU.subtract).then_inc(turned_lo[layer], 1)

            def row_max(b):
                dve.wait_ge(mm["energy"], b + 1)
                nc.vector.reduce_max(nmx[:, b, :], bank[where["energy", b]][:, :].rearrange("p (i s) -> p i s", i=2),
                                     AX.X, negate=True).then_inc(max_done, 1)

            def softmax_recip(b):
                dve.wait_ge(exp_done, b + 1)
                nc.vector.reciprocal(rsum[:, b, :], sums[:, b, :]).then_inc(rsum_done, 1)

            def softmax_norm(b):
                dve.wait_ge(rsum_done, b + 1)
                for i in range(2):
                    last = nc.vector.tensor_scalar(att[:, b, i, :], att[:, b, i, :], rsum[:, b, i:i + 1], None, ALU.mult)
                last.then_inc(att_done[b], 1)

            def q_clamp(n):
                dve.wait_ge(mm["q"], n + 1)
                if n >= 2:
                    dve.wait_ge(q_done, n - 1)
                nc.vector.tensor_scalar(eq[:, n % 2, :], bank[where["q", n]][:, :], qb[:, n % 2:n % 2 + 1], 0.0,
                                        ALU.add, ALU.min).then_inc(q_min[n], 1)

            def q_elu(n):
                if n == 0:
                    dve.wait_ge(ready, 1)
                dve.wait_ge(q_exp, n + 1)
                g, m = n // 2, n % 2
                nc.vector.scalar_tensor_tensor(out=qp[:, g, m, :], in0=bank[where["q", n]][:, :], scalar=qb1[:, m:m + 1],
                                               in1=eq[:, m, :], op0=ALU.add, op1=ALU.max).then_inc(q_done, 1)

            def kv_bias(t):
                if t == 0:
                    after("kvb")
                dve.wait_ge(mm["kv"], t + 1)
                nc.vector.tensor_tensor(kvs[:, t, :, 0:P], bank[where["kv", t]][:, :].rearrange("p (c w) -> p c w", w=P),
                                        kvb[:, :].rearrange("p (c w) -> p c w", w=P), ALU.add).then_inc(kv_done, 1)

            def k_elu(t):
                dve.wait_ge(k_exp, t + 1)
                k1 = kvs[:, t, 0:K, 0:P]
                nc.vector.scalar_tensor_tensor(out=k1, in0=ek[:, t % TG, :].rearrange("p (k c) -> p k c", k=K), scalar=1.0,
                                               in1=k1, op0=ALU.min, op1=ALU.max).then_inc(k_done, 1)

            def kv_blocks(b):
                dve.wait_ge(mm["kvm"], b + 1)
                src = bank[where["kvm", b]][:, 0:K * KVW].rearrange("p (k w) -> p k w", k=K)
                nc.vector.tensor_tensor(kvx[:, b, :, 0:P], src[:, :, 0:P],
                                        headmask.unsqueeze(1).to_broadcast([P, K, P]), ALU.mult)
                nc.vector.tensor_tensor(kvx[:, b, :, P:P + HC], src[:, :, P:P + 1].to_broadcast([P, K, HC]),
                                        headcols.unsqueeze(1).to_broadcast([P, K, HC]), ALU.mult).then_inc(kvx_done, 1)

            def attn_denominator(t):
                dve.wait_ge(mm["attn"], t + 1)
                src = bank[where["attn", t]][:, 0:K * (P + HC)].rearrange("p (k w) -> p k w", k=K)
                link(nc.vector.tensor_scalar(zs[:, t, :, :], src[:, :, P:P + HC], Z_EPS, None, ALU.add), ("arz", t))

            def attn_recip(t):
                after(("arz", t))
                link(nc.vector.reciprocal(rz[:, t, :, :], zs[:, t, :, :]), ("arr", t))

            def attn_rows(t):
                after(("arr", t))
                src = bank[where["attn", t]][:, 0:K * (P + HC)].rearrange("p (k w) -> p k w", k=K)
                nc.vector.tensor_tensor(ln[:, t, :].rearrange("p (k h e) -> p k h e", k=K, h=HC),
                                        src[:, :, 0:P].rearrange("p k (h e) -> p k h e", h=HC),
                                        rz[:, t, :, :].unsqueeze(3).to_broadcast([P, K, HC, HD]),
                                        ALU.mult).then_inc(attn_done, 1)

            def add_residual(kind, n, done):
                dve.wait_ge(mm[kind], n + 1)
                two = res[:, 2 * n:2 * n + 2, :].rearrange("p t c -> p (t c)")
                nc.vector.tensor_tensor(two, bank[where[kind, n]][:, :], two, ALU.add).then_inc(done, 1)

            def w2_low(n):
                dve.wait_ge(w2_hi, n + 1)
                dve.wait_ge(mm["w2h"], n + 1)
                nc.vector.scalar_tensor_tensor(out=w2[1][:, 2 * n:2 * n + 2, :].rearrange("p j d -> p (j d)"),
                                               in0=bank[where["w2h", n]][:, :], scalar=HAD_SCALE,
                                               in1=w2[0][:, 2 * n:2 * n + 2, :].rearrange("p j d -> p (j d)").bitcast(f32),
                                               op0=ALU.mult, op1=ALU.subtract).then_inc(w2_lo, 1)

            def hidden(i):
                dve.wait_ge(silu_done, i + 1)
                dve.wait_ge(mm["lin"], i + 1)
                if i >= 2:
                    dve.wait_ge(hid_hi, i - 1)
                    dve.wait_ge(hid_lo, i - 1)
                nc.vector.tensor_tensor(hid[:, i % 2, :], bank[where["lin", i]][:, :], gated[:, i % 2, :],
                                        ALU.mult).then_inc(hid_done, 1)

            def output(n, i):
                if n % 2 == 0:
                    dve.wait_ge(mm["acc"], n // 2 + 1)
                else:
                    dve.wait_ge(mm["down"], J * (n // 2 + 1))
                t = 2 * n + i
                nc.vector.tensor_tensor(res[:, t, :], bank[where["acc", n]][:, i * D:(i + 1) * D], res[:, t, :],
                                        ALU.add).then_inc(out_done, 1)

            def hidden_lo(i):
                dve.wait_ge(hid_done, i + 1)
                dve.wait_ge(hid_hi, i + 1)
                dve.wait_ge(mm["down"], i - 2)
                nc.vector.tensor_tensor(hs[1][:, i % 3, :], hid[:, i % 2, :], hs[0][:, i % 3, :],
                                        ALU.subtract).then_inc(hid_lo_last, 1)

            def consts(i):
                if i == 0:
                    link(nc.vector.memset(neg1[:, :], -1.0), "neg1")
                    dve.wait_ge(loaded["cols"], 16)
                    link(nc.vector.tensor_copy(had_r[:, :], had), "had")
                    link(nc.vector.tensor_scalar(nqb[:, :], qb, -1.0, None, ALU.mult), "nqb")
                    nc.vector.tensor_scalar(qb1[:, :], qb, 1.0, None, ALU.add).then_inc(ready, 1)
                if i == 1:
                    dve.wait_ge(loaded["rowb"], 16)
                    link(nc.vector.tensor_scalar(kvb[:, 0:D], kvb[:, 0:D], 1.0, None, ALU.add), "kvb")
                if i == 2:
                    dve.wait_ge(wqkv_lo, 2)
                    link(nc.vector.memset(kvs[:, :, K:2 * K, P:P + 1], 1.0), "ones")

            def add_output(n):
                if n % 2 == 0:
                    dve.wait_ge(xob_done, n // 2 + 1)
                add_residual("o", n, x1_done)

            row_stats(0, 0)
            consts(0)
            for i in range(1, 4):
                row_stats(0, i)
            for i in range(0, 3):
                row_scale(0, 0, i)
            for i in range(4, 7):
                row_stats(0, i)
            row_scale(0, 0, 3)
            row_stats(0, 7)
            row_scale(0, 0, 4)
            for i in range(5, 12):
                row_scale(0, 0, i)
                row_scale(0, 1, i - 5)
            normalize(0, 0)
            row_scale(0, 1, 7)
            for i in range(1, 4):
                normalize(0, i)
            row_scale(0, 1, 8)
            row_scale(0, 1, 9)
            row_max(0)
            turn_lo(0, 0)
            turn_lo(0, 1)
            consts(1)
            row_max(1)
            row_scale(0, 1, 10)
            row_scale(0, 1, 11)
            normalize(0, 4)
            row_max(2)
            normalize(0, 5)
            consts(2)
            normalize(0, 6)
            row_max(3)
            normalize(0, 7)
            q_elu(0)
            q_elu(1)
            kv_bias(0)
            kv_bias(1)
            k_elu(0)
            kv_bias(2)
            softmax_recip(0)
            k_elu(1)
            k_elu(2)
            softmax_recip(1)
            kv_bias(3)
            turn_lo(0, 2)
            k_elu(3)
            kv_blocks(0)
            turn_lo(0, 3)
            softmax_recip(2)
            kv_blocks(1)
            attn_denominator(0)
            attn_denominator(1)
            attn_recip(0)
            attn_denominator(2)
            attn_denominator(3)
            attn_rows(0)
            attn_recip(1)
            attn_rows(1)
            attn_recip(2)
            kv_bias(4)
            attn_rows(2)
            attn_recip(3)
            k_elu(4)
            attn_rows(3)
            q_clamp(2)
            kv_bias(5)
            softmax_recip(3)
            q_elu(2)
            q_clamp(3)
            q_elu(3)
            kv_bias(6)
            softmax_norm(3)
            add_output(0)
            k_elu(5)
            row_stats(1, 0)
            add_output(1)
            for i in range(1, 4):
                row_stats(1, i)
            w2_low(0)
            row_scale(1, 0, 0)
            kv_bias(7)
            for i in range(1, 5):
                row_scale(1, 0, i)
            k_elu(6)
            row_scale(1, 0, 5)
            kv_blocks(2)
            row_scale(1, 0, 6)
            k_elu(7)
            for i in range(7, 11):
                row_scale(1, 0, i)
            w2_low(1)
            row_scale(1, 0, 11)
            ln2_shift(0)
            w2_low(2)
            add_cross(0)
            row_stats(2, 0)
            row_stats(2, 1)
            add_cross(1)
            row_stats(2, 2)
            row_stats(2, 3)
            attn_denominator(4)
            row_scale(2, 0, 0)
            kv_blocks(3)
            attn_denominator(5)
            row_scale(2, 0, 1)
            attn_recip(4)
            row_scale(2, 0, 2)
            row_scale(2, 0, 3)
            attn_recip(5)
            row_scale(2, 0, 4)
            attn_denominator(6)
            row_scale(2, 0, 5)
            attn_recip(6)
            attn_denominator(7)
            row_scale(2, 0, 6)
            attn_rows(4)
            row_scale(2, 0, 7)
            attn_rows(5)
            attn_recip(7)
            row_scale(2, 0, 8)
            attn_rows(6)
            row_scale(2, 0, 9)
            attn_rows(7)
            row_scale(2, 0, 10)
            row_scale(2, 0, 11)
            for i in range(0, 4):
                normalize(2, i)
            add_output(2)
            row_stats(1, 4)
            turn_lo(2, 0)
            turn_lo(2, 1)
            add_output(3)
            row_stats(1, 5)
            row_stats(1, 6)
            w2_low(3)
            row_stats(1, 7)
            for i in range(0, 6):
                row_scale(1, 1, i)
            hidden(0)
            for i in range(6, 11):
                row_scale(1, 1, i)
            hidden(1)
            row_scale(1, 1, 11)
            ln2_shift(1)
            hidden(2)
            hidden(3)
            add_cross(2)
            add_cross(3)
            row_stats(2, 4)
            hidden(4)
            row_stats(2, 5)
            row_stats(2, 6)
            hidden(5)
            row_stats(2, 7)
            for i in range(0, 12):
                row_scale(2, 1, i)
            for i in range(4, 8):
                normalize(2, i)
            hidden(6)
            turn_lo(2, 2)
            turn_lo(2, 3)
            for i in range(7, 11):
                hidden(i)
            output(0, 0)
            output(0, 1)
            output(1, 0)
            output(1, 1)
            for i in range(11, 15):
                hidden(i)
            hidden_lo(14)
            hidden(15)
            hidden_lo(15)
            output(2, 0)
            output(2, 1)
            output(3, 0)
            output(3, 1)

        @block.tensor
        def _(pe):
            def claim(*unit):
                if before[unit] is not None:
                    pe.wait_ge(*emptied(before[unit]))
                return bank[where[unit]]

            def cross_projection(n):
                h, which = n // 2, n % 2
                ps = claim("xqk", n)
                if n % 2 == 0:
                    pe.wait_ge(loaded[f"ctx{h}"], 16)
                    pe.wait_ge(loaded["wxqk"], 16)
                nc.tensor.matmul(ps[:, :], wxq[:, which, :], ctx_sb[:, h * N:(h + 1) * N],
                                 start=True, stop=True).then_inc(mm["xqk"], 1)

            def energy(b):
                ps = claim("energy", b)
                pe.wait_ge(xqk_done, 2 * (b // 2) + 2)
                for i in range(2):
                    last = nc.tensor.matmul(ps[:, i * S:(i + 1) * S], xqk[:, b, 0, i * P:(i + 1) * P], xqk[:, b, 1, :],
                                            start=True, stop=True)
                last.then_inc(mm["energy"], 1)

            def turn_rows(stage, g, i):
                rows, rows_done, step = {"lnT0": (ln, normed.get((0, g)), 1), "aT": (ln, attn_done, 1), "lnT1": (res, x1_done, 2),
                                         "lnT2": (ln, normed.get((2, g)), 1)}[stage]
                if i == 0:
                    pair = [claim(stage, 2 * g + c) for c in range(K)]
                else:
                    pair = [bank[where[stage, 2 * g + c]] for c in range(K)]
                if stage == "lnT0" and g == 0:
                    pe.wait_ge(loaded["cols"], 16)
                for t in (2 * i, 2 * i + 1):
                    if step == 1 or t % 2 == 0:
                        pe.wait_ge(rows_done, t + 1 if stage in ("lnT0", "lnT2") else (g * TG + t) // step + 1)
                    for c in range(K):
                        last = nc.tensor.transpose(pair[c][:, t * P:(t + 1) * P],
                                                   rows[:, g * TG + t, c * P:(c + 1) * P], ident)
                        if t == TG - 1:
                            last.then_inc(mm[stage], 1)

            def turn_att(b):
                ps = claim("attT", b)
                pe.wait_ge(att_done[b], 1)
                for k in range(K):
                    for i in range(2):
                        last = nc.tensor.transpose(ps[:, k * S + i * P:k * S + (i + 1) * P],
                                                   att[:, b, i, k * P:(k + 1) * P], ident)
                last.then_inc(mm["attT"], 1)

            def query(n):
                g, m = n // 2, n % 2
                ps = claim("q", n)
                pe.wait_ge(turned_hi[0], 2 * g + 2)
                pe.wait_ge(turned_lo[0], 2 * g + 2)
                pe.wait_ge(wqkv_lo, 1)
                for i, (wp, xp) in enumerate(PARTS):
                    for k in range(K):
                        last = nc.tensor.matmul(ps[:, :], wqkv[wp][:, k, m * P:(m + 1) * P], lnT[xp][:, g, k, :],
                                                start=(i == 0 and k == 0), stop=(i == 2 and k == K - 1))
                last.then_inc(mm["q"], 1)

            def key_value(t):
                g, r = t // TG, t % TG
                ps = claim("kv", t)
                pe.wait_ge(turned_hi[0], 2 * g + 2)
                pe.wait_ge(turned_lo[0], 2 * g + 2)
                pe.wait_ge(wqkv_lo, 2)
                for i, (wp, xp) in enumerate(PARTS):
                    for k in range(K):
                        last = nc.tensor.matmul(ps[:, :], lnT[xp][:, g, k, r * P:(r + 1) * P], wqkv[wp][:, k, D:3 * D],
                                                start=(i == 0 and k == 0), stop=(i == 2 and k == K - 1))
                last.then_inc(mm["kv"], 1)

            def key_times_value(b):
                ps = claim("kvm", b)
                pe.wait_ge(k_done, 2 * b + 2)
                for c in range(K):
                    for i in range(2):
                        last = nc.tensor.matmul(ps[:, c * KVW:(c + 1) * KVW], kvs[:, 2 * b + i, c, 0:P],
                                                kvs[:, 2 * b + i, K + c, :], start=(i == 0), stop=(i == 1))
                last.then_inc(mm["kvm"], 1)

            def attention(t):
                g, r = t // TG, t % TG
                ps = claim("attn", t)
                pe.wait_ge(q_done, 2 * g + 2)
                pe.wait_ge(kvx_done, t // 2 + 1)
                W = P + HC
                for c in range(K):
                    last = nc.tensor.matmul(ps[:, c * W:(c + 1) * W], qp[:, g, c, r * P:(r + 1) * P],
                                            kvx[:, t // 2, c, :], start=True, stop=True)
                last.then_inc(mm["attn"], 1)

            def rows_times(stage, n, weights):
                ps = claim(stage, n)
                for i in range(2):
                    t = 2 * (n % 2) + i
                    for k in range(K):
                        last = nc.tensor.matmul(ps[:, i * D:(i + 1) * D], colT[:, n // 2, k, t * P:(t + 1) * P],
                                                weights(k), start=(k == 0), stop=(k == K - 1))
                last.then_inc(mm[stage], 1)

            def project(n):
                pe.wait_ge(aT_done, 2 * (n // 2) + 2)
                pe.wait_ge(loaded["ow"], 16)
                rows_times("o", n, lambda k: wo[:, k, :])

            def cross(n):
                pe.wait_ge(turned2, 2 * (n // 2) + 2)
                pe.wait_ge(attT_done, n + 1)
                rows_times("xm", n, lambda k: attT[:, n, k, :])

            def hadamard(n):
                ps = claim("w2h", n)
                pe.wait_ge(ready, 1)
                pe.wait_ge(w2s_hi, n + 1)
                pe.wait_ge(w2s_lo, n + 1)
                for part in (1, 0):
                    last = nc.tensor.matmul(ps[:, :], had_r[:, :], w2s[part][:, n % 2, :, :].rearrange("p j d -> p (j d)"),
                                            start=(part == 1), stop=(part == 0))
                last.then_inc(mm["w2h"], 1)

            def up(i, which):
                g, j = i // J, i % J
                if j == 0:
                    pe.wait_ge(turned_hi[2], 2 * g + 2)
                    pe.wait_ge(turned_lo[2], 2 * g + 2)
                if i == 0:
                    pe.wait_ge(w13_hi, 4)
                    pe.wait_ge(w13_lo, 4)
                for which, stage in ((which, ("gate", "lin")[which]),):
                    ps = claim(stage, i)
                    for n, (wp, xp) in enumerate(PARTS):
                        for k in range(K):
                            last = nc.tensor.matmul(ps[:, :], w13[wp][:, which, k, j * P:(j + 1) * P],
                                                    lnT[xp][:, g, k, :], start=(n == 0 and k == 0),
                                                    stop=(n == 2 and k == K - 1))
                    last.then_inc(mm[stage], 1)

            def down(i):
                g, j = i // J, i % J
                if j == 0:
                    for n in range(2):
                        claim("acc", 2 * g + n)
                if i == 0:
                    pe.wait_ge(w2_lo, 4)
                pe.wait_ge(hid_hi, i + 1)
                if i < G * J - LAST:
                    pe.wait_ge(hid_lo, i + 1)
                else:
                    pe.wait_ge(hid_lo_last, i - (G * J - LAST) + 1)
                for t in range(TG):
                    ps = bank[ACC[t // 2]][:, (t % 2) * D:(t % 2 + 1) * D]
                    for n, (wp, xp) in enumerate(PARTS):
                        last = nc.tensor.matmul(ps, hs[xp][:, i % 3, t * P:(t + 1) * P], w2[wp][:, j, :],
                                                start=(j == 0 and n == 0 and t % 2 == 0),
                                                stop=(j == J - 1 and n == 2 and t % 2 == 1), skip_group_check=True)
                    if j == J - 1 and t == 1:
                        last.then_inc(mm["acc"], 1)
                last.then_inc(mm["down"], 1)

            for i in range(0, 3):
                cross_projection(i)
            energy(0)
            energy(1)
            cross_projection(3)
            turn_rows("lnT0", 0, 0)
            turn_rows("lnT0", 0, 1)
            energy(2)
            energy(3)
            query(0)
            query(1)
            key_value(0)
            turn_rows("lnT0", 1, 0)
            key_value(1)
            key_value(2)
            turn_rows("lnT0", 1, 1)
            key_value(3)
            key_times_value(0)
            key_times_value(1)
            for i in range(0, 4):
                attention(i)
            for i in range(4, 6):
                key_value(i)
                turn_rows("aT", 0, i - 4)
                query(i - 2)
            key_value(6)
            project(0)
            project(1)
            hadamard(0)
            turn_att(0)
            key_value(7)
            key_times_value(2)
            turn_rows("lnT1", 0, 0)
            turn_rows("lnT1", 0, 1)
            hadamard(1)
            turn_att(1)
            hadamard(2)
            cross(0)
            cross(1)
            attention(4)
            key_times_value(3)
            turn_att(2)
            for i in range(5, 8):
                attention(i)
            turn_rows("aT", 1, 0)
            turn_att(3)
            turn_rows("aT", 1, 1)
            hadamard(3)
            turn_rows("lnT2", 0, 0)
            project(2)
            turn_rows("lnT2", 0, 1)
            project(3)
            turn_rows("lnT1", 1, 0)
            up(0, 0)
            turn_rows("lnT1", 1, 1)
            up(0, 1)
            up(1, 0)
            up(1, 1)
            up(2, 0)
            up(2, 1)
            down(0)
            up(3, 0)
            up(3, 1)
            up(4, 0)
            up(4, 1)
            cross(2)
            up(5, 0)
            cross(3)
            down(1)
            up(5, 1)
            up(6, 0)
            down(2)
            up(6, 1)
            down(3)
            up(7, 0)
            turn_rows("lnT2", 1, 0)
            turn_rows("lnT2", 1, 1)
            down(4)
            up(7, 1)
            up(8, 0)
            up(8, 1)
            down(5)
            up(9, 0)
            down(6)
            up(9, 1)
            up(10, 0)
            up(10, 1)
            down(7)
            up(11, 0)
            up(11, 1)
            up(12, 0)
            down(8)
            up(12, 1)
            up(13, 0)
            up(13, 1)
            up(14, 0)
            down(9)
            up(14, 1)
            down(10)
            up(15, 0)
            up(15, 1)
            for i in range(11, 16):
                down(i)


def kernel(**inputs):
    import numpy as np
    import concourse.bacc as bacc
    from concourse.bass_utils import run_bass_kernel_spmd

    P, HD, D = 128, 16, 256
    ones = np.ones((1, 1), np.float32)
    had = ones
    while had.shape[0] < P:
        had = np.block([[had, had], [had, -had]])
    heads = np.arange(P) // HD
    a = {n: np.asarray(v) for n, v in inputs.items()}
    cols = np.concatenate([
        np.eye(P, dtype=np.float32), had.astype(np.float32),
        (heads[:, None] == heads[None, :]).astype(np.float32),
        (heads[:, None] == np.arange(P // HD)[None, :]).astype(np.float32),
        a["L0_attn_q_b"].reshape(-1, P).T, a["L0_xattn_bq"].reshape(P, 1), a["L0_xattn_bk"].reshape(P, 1)], axis=1)
    arrays = {
        "x": a["x"].reshape(-1, D),
        "ctxT": a["ctx_1024"].reshape(-1, P).T,
        "q_wT": a["L0_attn_q_w"].T,
        "kv_wT": np.concatenate([a["L0_attn_k_w"].T, a["L0_attn_v_w"].T], axis=1),
        "o_wT": a["L0_attn_o_w"].T,
        "xqk_wT": np.concatenate([a["L0_xattn_Wq"].T, a["L0_xattn_Wk"].T], axis=1),
        "w1T": a["L0_ffn_W1"].T, "w3T": a["L0_ffn_W3"].T, "w2T": a["L0_ffn_W2"].T,
        "row_bias": np.concatenate([a["L0_attn_k_b"], a["L0_attn_v_b"], a["L0_attn_o_b"]]),
        "cols": cols,
    }
    arrays = {n: np.ascontiguousarray(v) for n, v in arrays.items()}
    nc = bacc.Bacc("TRN2", target_bir_lowering=False, num_devices=1)
    aps = [nc.dram_tensor(n, v.shape, mybir.dt.float32, kind="ExternalInput").ap() for n, v in arrays.items()]
    out = nc.dram_tensor("out", (a["x"].size // D, D), mybir.dt.float32, kind="ExternalOutput").ap()
    decoder_layer(nc, *aps, out)
    r = run_bass_kernel_spmd(nc, [arrays], core_ids=[0])
    return r.results[0]["out"].reshape(a["x"].shape)
```

```python
import concourse.bass as bass
from concourse import mybir
from contextlib import ExitStack


def decoder_layer(nc, x, ctxT, q_wT, kv_wT, o_wT, xqk_wT, w1T, w3T, w2T, row_bias, cols, out):
    f32, f32r, i32 = mybir.dt.float32, mybir.dt.float32r, mybir.dt.int32
    ALU, ACT, AX = mybir.AluOpType, mybir.ActivationFunctionType, mybir.AxisListType

    P = 128
    TOK, D = x.shape
    T = TOK // P
    B = 4
    S = TOK // B
    G, TG = 2, T // 2
    N = TG * P
    K = D // P
    HD = 16
    HC = P // HD
    H = w1T.shape[1]
    J = H // P
    LN_EPS, Z_EPS = 1e-5, 1e-6
    RSQRT_SEED = 0x5F3759DF
    HAD_SCALE = 1.0 / float(H) ** 0.5
    PARTS = ((1, 0), (0, 0), (0, 1))

    tiles = lambda ap: ap.rearrange("(t p) c -> p t c", p=P)

    ctx = ExitStack()
    with ctx:
        def sb(name, shape, dt=f32):
            return ctx.enter_context(nc.sbuf_tensor(name, shape, dt))

        def sem(name):
            return ctx.enter_context(nc.semaphore(name))

        res = sb("res", [P, T, D])
        ln = sb("ln", [P, T, D])
        lnT = [sb("lnT_hi", [P, G, K, N], f32r), sb("lnT_lo", [P, G, K, N], f32r)]
        colT = sb("colT", [P, K, N])
        qp = sb("qp", [P, G, K, N])
        eq = sb("eq", [P, K, N])
        KVW = P + 1
        kvs = sb("kvs", [P, T, 2 * K, KVW])
        ctx_sb = sb("ctx_sb", [P, TOK])
        ek = ctx_sb[:, :].rearrange("p (t c) -> p t c", c=D)
        wqkv = [sb("wqkv_hi", [P, K, 3 * D], f32r), sb("wqkv_lo", [P, K, 3 * D], f32r)]
        wqkv_raw = kvs[:, :, :, :].rearrange("p t c w -> p (t c w)")[:, 0:K * 3 * D].rearrange(
            "p (k n) -> p k n", k=K)
        wo = sb("wo", [P, K, D])
        colT1 = [w[:, :, :].rearrange("p k n -> p (k n)")[:, 0:K * N].rearrange("p (k n) -> p k n", k=K) for w in wqkv]
        wo_r = [w[:, :, :].rearrange("p k n -> p (k n)")[:, K * N:K * N + K * D].rearrange("p (k n) -> p k n", k=K)
                for w in wqkv]
        wxq = sb("wxq", [P, 2, P])
        xqk = sb("xqk", [P, B, 2, S])
        att = xqk
        attT = sb("attT", [P, 2, K, S])
        attT1 = [sb("attT1_hi", [P, 2, K, S], f32r), sb("attT1_lo", [P, 2, K, S], f32r)]
        w13_raw = sb("w13_raw", [P, 2, H])
        w13 = [sb("w13_hi", [P, 2, K, H], f32r), sb("w13_lo", [P, 2, K, H], f32r)]
        w2a = sb("w2a", [P, J, D])
        w2b = sb("w2b", [P, J, D])
        w2s = [sb("w2s_hi", [P, 2, 2, D], f32r), sb("w2s_lo", [P, 2, 2, D], f32r)]
        w2 = [sb("w2_hi", [P, J, D], f32r), sb("w2_lo", [P, J, D], f32r)]
        kvx = sb("kvx", [P, B, K, P + HC])
        gated = qp[:, 0, :, :]
        hid = eq
        hs = [sb("hid_hi", [P, 3, N], f32r), sb("hid_lo", [P, 3, N], f32r)]
        rowb = sb("rowb", [P, 3 * D])
        kvb, ob = rowb[:, 0:2 * D], rowb[:, 2 * D:3 * D]
        qb1 = sb("qb1", [P, K])
        cst = sb("cst", [P, 3 * P + HC + K + 2])
        ident, had, headmask = cst[:, 0:P], cst[:, P:2 * P], cst[:, 2 * P:3 * P]
        headcols = cst[:, 3 * P:3 * P + HC]
        qb, xqb = cst[:, 3 * P + HC:3 * P + HC + K], cst[:, 3 * P + HC + K:3 * P + HC + K + 2]
        had_r = sb("had_r", [P, P], f32r)
        stats = sb("stats", [P, 3, T, 6])
        mv = sb("mv", [P, 3, T, 2])
        ve = sb("ve", [P, 3, T])
        nt = sb("nt", [P, 3, T])
        rstd = sb("rstd", [P, 3, T])
        neg1 = sb("neg1", [P, 1])
        shift2 = sb("shift2", [P, T])
        nqb = sb("nqb", [P, K])
        sh = sb("sh", [P, 3, T])
        scrap = sb("scrap", [P, 1])
        nmx = sb("nmx", [P, B, 2])
        sums = sb("sums", [P, B, 2])
        rsum = sb("rsum", [P, B, 2])
        zs = sb("zs", [P, T, K, HC])
        rz = sb("rz", [P, T, K, HC])

        bank = [ctx.enter_context(nc.psum_tensor(f"bank{i}", [P, 512], f32)) for i in range(8)]
        ACC = (6, 7)
        LAST = 2
        where = {}
        before = {}
        last_in = [None] * 8

        def place(unit, b):
            where[unit], before[unit], last_in[b] = b, last_in[b], unit

        DMA_NAMES = ("x0a", "x0b", "x1", "cols", "ctx0", "ctx1", "wxqk", "qw", "kvw", "w2", "ow",
                     "w10", "w11", "w30", "w31", "rowb")
        loaded = {n: sem("loaded_" + n) for n in DMA_NAMES}
        mm = {n: sem("mm_" + n) for n in ("xqk", "lnT0", "lnT1", "lnT2", "energy", "q", "kv", "kvm", "attn",
                                          "aT", "attT", "o", "xm", "w2h", "gate", "lin", "down", "acc", "clock")}
        chain = sem("dve_chain")
        normed = {(m, g): sem(f"ln{m + 1}_rows{g}") for m in (0, 2) for g in range(G)}
        scaled = {(m, g): sem(f"ln{m + 1}_scale{g}") for m in (0, 2) for g in range(G)}
        rsum_done = sem("rsum_done")
        scale2 = sem("ln2_scale")
        shifted2 = sem("ln2_shifted")
        turned_hi = {0: sem("ln1T_hi"), 2: sem("ln3T_hi")}
        turned_lo = {0: sem("ln1T_lo"), 2: sem("ln3T_lo")}
        turned2 = sem("ln2T")
        xqk_done = sem("xqk_done")
        max_done = sem("max_done")
        exp_done = sem("exp_done")
        att_done = [sem(f"att_done{b}") for b in range(B)]
        attT_done = sem("attT_done")
        q_min = [sem(f"q_min{n}") for n in range(G * K)]
        q_exp = sem("q_exp")
        q_done = sem("q_done")
        kv_done = sem("kv_done")
        k_exp = sem("k_exp")
        k_done = sem("k_done")
        kvx_done = sem("kvx_done")
        attn_done = sem("attn_done")
        aT_done = sem("aT_done")
        xob_done = sem("xob_done")
        x1_done = sem("x1_done")
        x2_done = sem("x2_done")
        aT_lo, turned2_lo, attT_lo = sem("aT_lo"), sem("ln2T_lo"), sem("attT_lo")
        wo_hi, wo_lo = sem("wo_hi_done"), sem("wo_lo_done")
        zeroed = sem("zeroed")
        table_done = sem("table_done")
        ready = sem("ready")
        wqkv_hi = sem("wqkv_hi_done")
        wqkv_lo = sem("wqkv_lo_done")
        w13_hi = sem("w13_hi_done")
        w13_lo = sem("w13_lo_done")
        fly = sem("w2_butterfly")
        w2s_hi = sem("w2s_hi_done")
        w2s_lo = sem("w2s_lo_done")
        w2_hi = sem("w2_hi_done")
        w2_lo = sem("w2_lo_done")
        silu_done = sem("silu_done")
        hid_done = sem("hid_done")
        hid_hi = sem("hid_hi_done")
        hid_lo_last = sem("hid_lo_last_done")
        hid_lo = sem("hid_lo_done")
        out_done = sem("out_done")
        stored = sem("stored")

        def emptied(unit):
            kind, n = unit
            if kind in ("aT", "lnT1", "attT") and n >= 2:
                return {"aT": aT_lo, "lnT1": turned2_lo, "attT": attT_lo}[kind], n - 1
            return {"xqk": xqk_done, "lnT0": turned_lo[0], "lnT1": turned2, "lnT2": turned_lo[2],
                    "energy": exp_done, "q": q_done, "kv": kv_done, "kvm": kvx_done, "attn": attn_done,
                    "aT": aT_done, "attT": attT_done, "o": x1_done, "xm": x2_done, "w2h": w2_lo,
                    "clock": mm["clock"], "gate": silu_done, "lin": hid_done,
                    "acc": out_done}[kind], {"xm": 2 * n + 2, "acc": 2 * n + 2, "clock": 1}.get(kind, n + 1)

        BANKS = (
            (("xqk", 0), ("energy", 2), ("lnT0", 3), ("attn", 1), ("o", 0), ("xm", 1), ("w2h", 0),),
            (("xqk", 1), ("energy", 3), ("q", 1), ("attn", 2), ("o", 1), ("kvm", 3), ("attT", 2),),
            (("xqk", 2), ("kv", 0), ("attT", 0), ("attn", 3), ("lnT1", 0), ("attn", 4), ("attT", 3),),
            (("xqk", 3), ("q", 0), ("kvm", 0), ("kv", 6), ("lnT1", 1), ("attn", 5), ("lnT2", 0), ("o", 3), ("xm", 2),
             ("lnT2", 2),),
            (("energy", 0), ("kv", 1), ("kv", 4), ("aT", 0), ("q", 2), ("attn", 6), ("lnT2", 1), ("lnT1", 2),
             ("xm", 3), ("lnT2", 3),),
            (("energy", 1), ("kv", 2), ("kv", 5), ("aT", 1), ("q", 3), ("attn", 7), ("w2h", 1), ("lnT1", 3),
             ("w2h", 3),),
            (("lnT0", 0), ("kv", 3), ("kvm", 1), ("attT", 1), ("kvm", 2), ("aT", 2), ("w2h", 2),),
            (("lnT0", 1), ("lnT0", 2), ("attn", 0), ("kv", 7), ("xm", 0), ("aT", 3), ("o", 2),),
        )
        place(("clock", 7), 7)
        for b, units in enumerate(BANKS):
            for unit in units:
                place(unit, b)
        for i in range(G * J):
            place(("gate", i), (2 * i) % 3)
            place(("lin", i), (2 * i + 1) % 3)
        for n in range(2 * G):
            place(("acc", n), ACC[n % 2])

        block = ctx.enter_context(nc.Block())

        xt = tiles(x)

        def do_load(q, nm):
            if nm in ("w10", "w11", "w30", "w31"):
                n = ("w10", "w11", "w30", "w31").index(nm)
                if n >= 2:
                    q.wait_ge(w13_lo, n - 1)
                    q.wait_ge(w13_hi, n - 1)
                w, k = (w1T, w3T)[n // 2], n % 2
                q.dma_start(w13_raw[:, n % 2, :], w[k * P:(k + 1) * P, :]).then_inc(loaded[nm], 16)
                return
            dst, src = {
                "x0a": (res[:, 0:2, :], xt[:, 0:2, :]), "x0b": (res[:, 2:TG, :], xt[:, 2:TG, :]),
                "x1": (res[:, TG:T, :], xt[:, TG:T, :]),
                "qw": (wqkv_raw[:, :, 0:D], q_wT.rearrange("(k p) n -> p k n", p=P)),
                "kvw": (wqkv_raw[:, :, D:3 * D], kv_wT.rearrange("(k p) n -> p k n", p=P)),
                "w2": (w2a[:, :, :], w2T.rearrange("(j p) d -> p j d", p=P)),
                "ow": (wo[:, :, :], o_wT.rearrange("(k p) n -> p k n", p=P)),
                "wxqk": (wxq[:, :, :], xqk_wT.rearrange("c (w d) -> c w d", w=2)),
                "ctx0": (ctx_sb[:, 0:N], ctxT[:, 0:N]), "ctx1": (ctx_sb[:, N:TOK], ctxT[:, N:TOK]),
                "cols": (cst[:, :], cols), "rowb": (rowb[:, :], row_bias.partition_broadcast(P))}[nm]
            q.dma_start(dst, src).then_inc(loaded[nm], 16)

        @block.sync
        def _(sp):
            for nm in ("wxqk", "ctx0", "x0a", "x0b", "qw", "ctx1", "cols", "kvw", "x1", "rowb", "w11", "w2", "w10", "w30", "w31", "ow"):
                do_load(sp, nm)
            ot = tiles(out)
            for n in range(2 * G - 1):
                sp.wait_ge(out_done, 2 * n + 2)
                sp.dma_start(ot[:, 2 * n:2 * n + 2, :], res[:, 2 * n:2 * n + 2, :]).then_inc(stored, 16)
            for t in (T - 2, T - 1):
                sp.wait_ge(out_done, t + 1)
                sp.dma_start(ot[:, t:t + 1, :], res[:, t:t + 1, :]).then_inc(stored, 16)
            sp.wait_ge(stored, (2 * G + 1) * 16)

        @block.gpsimd
        def _(pool):
            def split_qkv(i):
                n, s = (("qw", slice(0, D)), ("kvw", slice(D, 3 * D)))[i]
                pool.wait_ge(loaded[n], 16)
                pool.wait_ge(wqkv_hi, i + 1)
                nc.gpsimd.tensor_tensor(wqkv[1][:, :, s], wqkv_raw[:, :, s], wqkv[0][:, :, s],
                                        ALU.subtract).then_inc(wqkv_lo, 1)

            def residual_bias(g):
                pool.wait_ge(loaded["rowb"], 16)
                pool.wait_ge(normed[0, g], TG)
                half = res[:, g * TG:(g + 1) * TG, :]
                nc.gpsimd.tensor_tensor(half, half, ob[:, :].unsqueeze(1).to_broadcast([P, TG, D]),
                                        ALU.add).then_inc(xob_done, 1)

            def butterfly(n):
                s, which = n // 2, n % 2
                step = (1, 2, 4)[s]
                src, dst = ((w2a, w2b), (w2b, w2a))[s % 2]
                if n == 0:
                    pool.wait_ge(loaded["w2"], 16)
                if s and which == 0:
                    pool.wait_ge(fly, 2 * s)
                a = src[:, :, :].rearrange("p (u two v) d -> p u two (v d)", two=2, v=step)
                o = dst[:, :, :].rearrange("p (u two v) d -> p u two (v d)", two=2, v=step)
                nc.gpsimd.tensor_tensor(o[:, :, which, :], a[:, :, 0, :], a[:, :, 1, :],
                                        (ALU.add, ALU.subtract)[which]).then_inc(fly, 1)

            def split_w13(m):
                pool.wait_ge(loaded[("w10", "w11", "w30", "w31")[m]], 16)
                pool.wait_ge(w13_hi, m + 1)
                nc.gpsimd.tensor_tensor(w13[1][:, m // 2, m % 2, :], w13_raw[:, m % 2, :],
                                        w13[0][:, m // 2, m % 2, :], ALU.subtract).then_inc(w13_lo, 1)

            def split_w2(n):
                pool.wait_ge(w2s_hi, n + 1)
                if n >= 2:
                    pool.wait_ge(mm["w2h"], n - 1)
                nc.gpsimd.tensor_tensor(w2s[1][:, n % 2, :, :], w2b[:, 2 * n:2 * n + 2, :], w2s[0][:, n % 2, :, :],
                                        ALU.subtract).then_inc(w2s_lo, 1)

            def hidden_lo(i):
                pool.wait_ge(hid_done, i + 1)
                pool.wait_ge(hid_hi, i + 1)
                if i >= 3:
                    pool.wait_ge(mm["down"], i - 2)
                nc.gpsimd.tensor_tensor(hs[1][:, i % 3, :], hid[:, i % 2, :], hs[0][:, i % 3, :],
                                        ALU.subtract).then_inc(hid_lo, 1)

            split_qkv(0)
            split_qkv(1)
            residual_bias(0)
            butterfly(0)
            butterfly(1)
            split_w13(0)
            split_w13(1)
            butterfly(2)
            residual_bias(1)
            butterfly(3)
            split_w13(2)
            butterfly(4)
            butterfly(5)
            split_w13(3)
            for i in range(0, 4):
                split_w2(i)
            for i in range(0, 14):
                hidden_lo(i)

        @block.scalar
        def _(act):
            for nm in ():
                do_load(act, nm)

            def copy(dst, src, done):
                nc.scalar.activation(dst, src, ACT.Copy).then_inc(done, 1)

            def load_exp_table():
                act.wait_ge(zeroed, 1)
                nc.scalar.activation(scrap[:, :], eq[:, 0, 0:1], ACT.Exp).then_inc(table_done, 1)

            def split_qkv(i):
                n, part = (("qw", slice(0, D)), ("kvw", slice(D, 3 * D)))[i]
                act.wait_ge(loaded[n], 16)
                copy(wqkv[0][:, :, part], wqkv_raw[:, :, part], wqkv_hi)

            def cross_projection(n):
                act.wait_ge(mm["xqk"], n + 1)
                if n == 0:
                    act.wait_ge(loaded["cols"], 16)
                h, which = n // 2, n % 2
                nc.scalar.activation(xqk[:, 2 * h:2 * h + 2, which, :],
                                     bank[where["xqk", n]][:, :].rearrange("p (b s) -> p b s", b=2),
                                     ACT.Identity, bias=xqb[:, which:which + 1]).then_inc(xqk_done, 1)

            def softmax_exp(b):
                act.wait_ge(max_done, b + 1)
                for i in range(2):
                    last = nc.scalar.activation(att[:, b, i, :], bank[where["energy", b]][:, i * S:(i + 1) * S],
                                                ACT.Exp, bias=nmx[:, b, i:i + 1], accum_out=sums[:, b, i:i + 1])
                last.then_inc(exp_done, 1)

            def turn_hi(layer, n):
                act.wait_ge(mm[f"lnT{layer}"], n + 1)
                copy(lnT[0][:, n // 2, n % 2, :], bank[where[f"lnT{layer}", n]][:, :], turned_hi[layer])

            def turn_2(n):
                act.wait_ge(mm["lnT1"], n + 1)
                copy((colT if n < 2 else colT1[0])[:, n % 2, :], bank[where["lnT1", n]][:, :], turned2)

            def shift_row(t):
                act.wait_ge(scale2, t // TG + 1)
                nc.scalar.activation(ln[:, t, :], res[:, t, :], ACT.Identity,
                                     bias=shift2[:, t:t + 1]).then_inc(shifted2, 1)

            def turn_attn(n):
                act.wait_ge(mm["aT"], n + 1)
                copy((colT if n < 2 else colT1[0])[:, n % 2, :], bank[where["aT", n]][:, :], aT_done)

            def turn_att(b):
                act.wait_ge(mm["attT"], b + 1)
                copy((attT if b < 2 else attT1[0])[:, b % 2, :, :].rearrange("p k s -> p (k s)"),
                     bank[where["attT", b]][:, :], attT_done)

            def q_exponential(n):
                act.wait_ge(q_min[n], 1)
                nc.scalar.activation(eq[:, n % 2, :], eq[:, n % 2, :], ACT.Exp,
                                     scale=-1.0).then_inc(q_exp, 1)

            def q_clamp(n):
                act.wait_ge(mm["q"], n + 1)
                act.wait_ge(ready, 1)
                if n >= 2:
                    act.wait_ge(q_done, n - 1)
                nc.scalar.activation(eq[:, n % 2, :], bank[where["q", n]][:, :], ACT.Relu, scale=-1.0,
                                     bias=nqb[:, n % 2:n % 2 + 1]).then_inc(q_min[n], 1)

            def softmax_norm(b):
                act.wait_ge(rsum_done, b + 1)
                for i in range(2):
                    last = nc.scalar.activation(att[:, b, i, :], att[:, b, i, :], ACT.Copy, scale=rsum[:, b, i:i + 1])
                last.then_inc(att_done[b], 1)

            def k_exponential(t):
                act.wait_ge(kv_done, t + 1)
                if t >= TG:
                    act.wait_ge(k_done, t - TG + 1)
                nc.scalar.activation(ek[:, t % TG, :].rearrange("p (k c) -> p k c", k=K), kvs[:, t, 0:K, 0:P], ACT.Exp,
                                     bias=neg1[:, 0:1]).then_inc(k_exp, 1)

            def split_w13(m):
                act.wait_ge(loaded[("w10", "w11", "w30", "w31")[m]], 16)
                copy(w13[0][:, m // 2, m % 2, :], w13_raw[:, m % 2, :], w13_hi)

            def split_wo():
                act.wait_ge(loaded["ow"], 16)
                act.wait_ge(mm["kv"], T)
                copy(wo_r[0][:, :, :], wo[:, :, :], wo_hi)

            def split_w2(n):
                act.wait_ge(fly, 6)
                if n >= 2:
                    act.wait_ge(mm["w2h"], n - 1)
                    act.wait_ge(w2s_lo, n - 1)
                copy(w2s[0][:, n % 2, :, :], w2b[:, 2 * n:2 * n + 2, :], w2s_hi)

            def turned_w2(n):
                act.wait_ge(mm["w2h"], n + 1)
                nc.scalar.activation(w2[0][:, 2 * n:2 * n + 2, :].rearrange("p j d -> p (j d)"),
                                     bank[where["w2h", n]][:, :], ACT.Copy, scale=HAD_SCALE).then_inc(w2_hi, 1)

            def silu(i):
                act.wait_ge(mm["gate"], i + 1)
                if i >= 2:
                    act.wait_ge(hid_done, i - 1)
                nc.scalar.activation(gated[:, i % 2, :], bank[where["gate", i]][:, :], ACT.Silu).then_inc(silu_done, 1)

            def hidden_hi(i):
                act.wait_ge(hid_done, i + 1)
                if i >= 3:
                    act.wait_ge(mm["down"], i - 2)
                copy(hs[0][:, i % 3, :], hid[:, i % 2, :], hid_hi)

            load_exp_table()
            split_qkv(0)
            for i in range(0, 3):
                cross_projection(i)
            split_qkv(1)
            cross_projection(3)
            turn_hi(0, 0)
            turn_hi(0, 1)
            for i in range(0, 3):
                softmax_exp(i)
            q_clamp(0)
            softmax_exp(3)
            q_exponential(0)
            k_exponential(0)
            softmax_norm(0)
            k_exponential(1)
            split_w13(0)
            k_exponential(2)
            q_clamp(1)
            turn_hi(0, 2)
            turn_hi(0, 3)
            q_exponential(1)
            k_exponential(3)
            split_w13(1)
            turn_att(0)
            k_exponential(4)
            split_w13(2)
            softmax_norm(1)
            k_exponential(5)
            turn_attn(0)
            turn_attn(1)
            split_w13(3)
            split_wo()
            k_exponential(6)
            softmax_norm(2)
            k_exponential(7)
            softmax_norm(3)
            turn_att(1)
            turn_2(0)
            q_clamp(2)
            turn_2(1)
            q_exponential(2)
            q_clamp(3)
            q_exponential(3)
            shift_row(0)
            shift_row(1)
            split_w2(0)
            shift_row(2)
            shift_row(3)
            split_w2(1)
            turned_w2(0)
            split_w2(2)
            turn_attn(2)
            turn_attn(3)
            turn_att(2)
            turn_hi(2, 0)
            turn_hi(2, 1)
            turned_w2(1)
            turned_w2(2)
            turn_att(3)
            silu(0)
            turn_2(2)
            split_w2(3)
            hidden_hi(0)
            turn_2(3)
            silu(1)
            for i in range(4, 7):
                shift_row(i)
            hidden_hi(1)
            silu(2)
            shift_row(7)
            turned_w2(3)
            for i in range(3, 7):
                silu(i)
                hidden_hi(i - 1)
            turn_hi(2, 2)
            hidden_hi(6)
            turn_hi(2, 3)
            silu(7)
            hidden_hi(7)
            silu(8)
            silu(9)
            hidden_hi(8)
            hidden_hi(9)
            silu(10)
            hidden_hi(10)
            silu(11)
            for i in range(12, 15):
                silu(i)
                hidden_hi(i - 1)
            hidden_hi(14)
            silu(15)
            hidden_hi(15)

        @block.vector
        def _(dve):
            links = [0]
            mark = {}

            def link(ins, name):
                links[0] += 1
                mark[name] = links[0]
                ins.then_inc(chain, 1)

            def after(name):
                dve.wait_ge(chain, mark[name])

            def row_stats(layer, t):
                g = t // TG
                if layer == 0 and t in (0, 2, 4):
                    dve.wait_ge(loaded[{0: "x0a", 2: "x0b", 4: "x1"}[t]], 16)
                if layer == 1 and t % 2 == 0:
                    dve.wait_ge(x1_done, t // 2 + 1)
                if layer == 2:
                    dve.wait_ge(x2_done, t + 1)
                link(nc.vector.bn_stats(stats[:, layer, t, :], res[:, t, :]), ("bn", layer, t))

            def row_scale(layer, g, s):
                own = slice(g * TG, (g + 1) * TG)
                y, h, v = rstd[:, layer, own], nt[:, layer, own], ve[:, layer, own]
                me, pr = ("rs", layer, g, s), ("rs", layer, g, s - 1)
                if s == 0:
                    after(("bn", layer, g * TG + TG - 1))
                    for t in range(g * TG, (g + 1) * TG):
                        link(nc.vector.bn_aggr(mv[:, layer, t, :], stats[:, layer, t, :]), me)
                    return
                after(pr)
                if s == 11:
                    nc.vector.scalar_tensor_tensor(out=sh[:, layer, own], in0=mv[:, layer, own, 0], scalar=-1.0,
                                                   in1=y, op0=ALU.mult, op1=ALU.mult).then_inc(scaled[layer, g], 1)
                elif s == 1:
                    link(nc.vector.tensor_scalar(v, mv[:, layer, own, 1], LN_EPS, None, ALU.add), me)
                elif s == 2:
                    link(nc.vector.tensor_scalar(y.bitcast(i32), v.bitcast(i32), -0.5, RSQRT_SEED,
                                                 ALU.mult, ALU.add), me)
                elif s in (3, 6):
                    link(nc.vector.tensor_tensor(h, y, y, ALU.mult), me)
                elif s == 4:
                    link(nc.vector.scalar_tensor_tensor(out=h, in0=h, scalar=-0.5, in1=v,
                                                        op0=ALU.mult, op1=ALU.mult), me)
                elif s == 5:
                    link(nc.vector.scalar_tensor_tensor(out=y, in0=h, scalar=1.5, in1=y,
                                                        op0=ALU.add, op1=ALU.mult), me)
                elif s == 7:
                    link(nc.vector.tensor_tensor(v, h, v, ALU.mult), me)
                elif s == 8:
                    link(nc.vector.tensor_scalar(h, v, 0.375, -1.25, ALU.mult, ALU.add), me)
                elif s == 9:
                    link(nc.vector.tensor_tensor(h, h, v, ALU.mult), me)
                else:
                    link(nc.vector.scalar_tensor_tensor(out=y, in0=h, scalar=1.875, in1=y,
                                                        op0=ALU.add, op1=ALU.mult), me)

            def normalize(layer, t):
                after(("rs", layer, t // TG, 10))
                nc.vector.tensor_scalar(ln[:, t, :], res[:, t, :], mv[:, layer, t, 0:1], rstd[:, layer, t:t + 1],
                                        ALU.subtract, ALU.mult).then_inc(normed[layer, t // TG], 1)

            def ln2_shift(g):
                after(("rs", 1, g, 10))
                own = slice(g * TG, (g + 1) * TG)
                nc.vector.scalar_tensor_tensor(out=shift2[:, own], in0=mv[:, 1, own, 0], scalar=-1.0,
                                               in1=rstd[:, 1, own], op0=ALU.mult, op1=ALU.mult).then_inc(scale2, 1)

            def add_cross(n):
                dve.wait_ge(mm["xm"], n + 1)
                for i in range(2):
                    t = 2 * n + i
                    dve.wait_ge(shifted2, t + 1)
                    nc.vector.scalar_tensor_tensor(out=res[:, t, :], in0=bank[where["xm", n]][:, i * D:(i + 1) * D],
                                                   scalar=rstd[:, 1, t:t + 1], in1=ln[:, t, :],
                                                   op0=ALU.mult, op1=ALU.add).then_inc(x2_done, 1)

            def turn_lo(layer, n):
                dve.wait_ge(turned_hi[layer], n + 1)
                dve.wait_ge(mm[f"lnT{layer}"], n + 1)
                nc.vector.tensor_tensor(lnT[1][:, n // 2, n % 2, :], bank[where[f"lnT{layer}", n]][:, :],
                                        lnT[0][:, n // 2, n % 2, :].bitcast(f32),
                                        ALU.subtract).then_inc(turned_lo[layer], 1)

            def row_max(b):
                dve.wait_ge(mm["energy"], b + 1)
                nc.vector.reduce_max(nmx[:, b, :], bank[where["energy", b]][:, :].rearrange("p (i s) -> p i s", i=2),
                                     AX.X, negate=True).then_inc(max_done, 1)

            def softmax_recip(b):
                dve.wait_ge(exp_done, b + 1)
                nc.vector.reciprocal(rsum[:, b, :], sums[:, b, :]).then_inc(rsum_done, 1)


            def q_elu(n):
                if n == 0:
                    dve.wait_ge(ready, 1)
                dve.wait_ge(q_exp, n + 1)
                g, m = n // 2, n % 2
                nc.vector.scalar_tensor_tensor(out=qp[:, g, m, :], in0=bank[where["q", n]][:, :],
                                               scalar=qb1[:, m:m + 1], in1=eq[:, m, :], op0=ALU.add, op1=ALU.max).then_inc(q_done, 1)

            def kv_bias(t):
                if t == 0:
                    after("kvb")
                dve.wait_ge(mm["kv"], t + 1)
                nc.vector.tensor_tensor(kvs[:, t, :, 0:P], bank[where["kv", t]][:, :].rearrange("p (c w) -> p c w", w=P),
                                        kvb[:, :].rearrange("p (c w) -> p c w", w=P), ALU.add).then_inc(kv_done, 1)

            def k_elu(t):
                dve.wait_ge(k_exp, t + 1)
                k1 = kvs[:, t, 0:K, 0:P]
                nc.vector.scalar_tensor_tensor(out=k1, in0=ek[:, t % TG, :].rearrange("p (k c) -> p k c", k=K), scalar=1.0,
                                               in1=k1, op0=ALU.min, op1=ALU.max).then_inc(k_done, 1)

            def kv_blocks(b):
                dve.wait_ge(mm["kvm"], b + 1)
                src = bank[where["kvm", b]][:, 0:K * KVW].rearrange("p (k w) -> p k w", k=K)
                nc.vector.tensor_tensor(kvx[:, b, :, 0:P], src[:, :, 0:P],
                                        headmask.unsqueeze(1).to_broadcast([P, K, P]), ALU.mult)
                nc.vector.tensor_tensor(kvx[:, b, :, P:P + HC], src[:, :, P:P + 1].to_broadcast([P, K, HC]),
                                        headcols.unsqueeze(1).to_broadcast([P, K, HC]), ALU.mult).then_inc(kvx_done, 1)

            def attn_denominator(t):
                dve.wait_ge(mm["attn"], t + 1)
                src = bank[where["attn", t]][:, 0:K * (P + HC)].rearrange("p (k w) -> p k w", k=K)
                link(nc.vector.tensor_scalar(zs[:, t, :, :], src[:, :, P:P + HC], Z_EPS, None, ALU.add), ("arz", t))

            def attn_recip(t):
                after(("arz", t))
                link(nc.vector.reciprocal(rz[:, t, :, :], zs[:, t, :, :]), ("arr", t))

            def attn_rows(t):
                after(("arr", t))
                src = bank[where["attn", t]][:, 0:K * (P + HC)].rearrange("p (k w) -> p k w", k=K)
                nc.vector.tensor_tensor(ln[:, t, :].rearrange("p (k h e) -> p k h e", k=K, h=HC),
                                        src[:, :, 0:P].rearrange("p k (h e) -> p k h e", h=HC),
                                        rz[:, t, :, :].unsqueeze(3).to_broadcast([P, K, HC, HD]),
                                        ALU.mult).then_inc(attn_done, 1)

            def add_residual(kind, n, done):
                dve.wait_ge(mm[kind], n + 1)
                two = res[:, 2 * n:2 * n + 2, :].rearrange("p t c -> p (t c)")
                nc.vector.tensor_tensor(two, bank[where[kind, n]][:, :], two, ALU.add).then_inc(done, 1)

            def split_wo():
                dve.wait_ge(wo_hi, 1)
                nc.vector.tensor_tensor(wo_r[1][:, :, :], wo[:, :, :], wo_r[0][:, :, :].bitcast(f32),
                                        ALU.subtract).then_inc(wo_lo, 1)

            def rows_lo(kind, n):
                hi_done, lo_done = {"aT": (aT_done, aT_lo), "lnT1": (turned2, turned2_lo)}[kind]
                dve.wait_ge(hi_done, n + 1)
                dve.wait_ge(mm[kind], n + 1)
                nc.vector.tensor_tensor(colT1[1][:, n % 2, :], bank[where[kind, n]][:, :],
                                        colT1[0][:, n % 2, :].bitcast(f32), ALU.subtract).then_inc(lo_done, 1)

            def att_lo(b):
                dve.wait_ge(attT_done, b + 1)
                dve.wait_ge(mm["attT"], b + 1)
                flat = lambda ap: ap[:, b % 2, :, :].rearrange("p k s -> p (k s)")
                nc.vector.tensor_tensor(flat(attT1[1]), bank[where["attT", b]][:, :], flat(attT1[0]).bitcast(f32),
                                        ALU.subtract).then_inc(attT_lo, 1)

            def w2_low(n):
                dve.wait_ge(w2_hi, n + 1)
                dve.wait_ge(mm["w2h"], n + 1)
                nc.vector.scalar_tensor_tensor(out=w2[1][:, 2 * n:2 * n + 2, :].rearrange("p j d -> p (j d)"),
                                               in0=bank[where["w2h", n]][:, :], scalar=HAD_SCALE,
                                               in1=w2[0][:, 2 * n:2 * n + 2, :].rearrange("p j d -> p (j d)").bitcast(f32),
                                               op0=ALU.mult, op1=ALU.subtract).then_inc(w2_lo, 1)

            def hidden(i):
                dve.wait_ge(silu_done, i + 1)
                dve.wait_ge(mm["lin"], i + 1)
                if i >= 2:
                    dve.wait_ge(hid_hi, i - 1)
                    dve.wait_ge(hid_lo, i - 1)
                nc.vector.tensor_tensor(hid[:, i % 2, :], bank[where["lin", i]][:, :], gated[:, i % 2, :],
                                        ALU.mult).then_inc(hid_done, 1)

            def output(n, i):
                if n % 2 == 0:
                    dve.wait_ge(mm["acc"], n // 2 + 1)
                else:
                    dve.wait_ge(mm["down"], J * (n // 2 + 1))
                t = 2 * n + i
                nc.vector.tensor_tensor(res[:, t, :], bank[where["acc", n]][:, i * D:(i + 1) * D], res[:, t, :],
                                        ALU.add).then_inc(out_done, 1)

            def hidden_lo(i):
                dve.wait_ge(hid_done, i + 1)
                dve.wait_ge(hid_hi, i + 1)
                dve.wait_ge(mm["down"], i - 2)
                nc.vector.tensor_tensor(hs[1][:, i % 3, :], hid[:, i % 2, :], hs[0][:, i % 3, :],
                                        ALU.subtract).then_inc(hid_lo_last, 1)

            def consts(i):
                if i == 3:
                    nc.vector.memset(eq[:, 0, 0:P], 0.0).then_inc(zeroed, 1)
                if i == 0:
                    link(nc.vector.memset(neg1[:, :], -1.0), "neg1")
                    dve.wait_ge(loaded["cols"], 16)
                    link(nc.vector.tensor_copy(had_r[:, :], had), "had")
                    link(nc.vector.tensor_scalar(nqb[:, :], qb, -1.0, None, ALU.mult), "nqb")
                    nc.vector.tensor_scalar(qb1[:, :], qb, 1.0, None, ALU.add).then_inc(ready, 1)
                if i == 1:
                    dve.wait_ge(loaded["rowb"], 16)
                    link(nc.vector.tensor_scalar(kvb[:, 0:D], kvb[:, 0:D], 1.0, None, ALU.add), "kvb")
                if i == 2:
                    dve.wait_ge(wqkv_lo, 2)
                    link(nc.vector.memset(kvs[:, :, K:2 * K, P:P + 1], 1.0), "ones")

            def add_output(n):
                if n % 2 == 0:
                    dve.wait_ge(xob_done, n // 2 + 1)
                add_residual("o", n, x1_done)

            consts(3)
            for i in range(0, 4):
                row_stats(0, i)
            for i in range(0, 8):
                row_scale(0, 0, i)
            consts(0)
            for i in range(8, 11):
                row_scale(0, 0, i)
            for i in range(0, 3):
                normalize(0, i)
            row_max(0)
            normalize(0, 3)
            row_stats(0, 4)
            row_max(1)
            for i in range(5, 8):
                row_stats(0, i)
            turn_lo(0, 0)
            turn_lo(0, 1)
            row_scale(0, 1, 0)
            row_max(2)
            row_scale(0, 1, 1)
            row_max(3)
            softmax_recip(0)
            for i in range(2, 5):
                row_scale(0, 1, i)
            consts(1)
            row_scale(0, 1, 5)
            consts(2)
            softmax_recip(1)
            row_scale(0, 1, 6)
            row_scale(0, 1, 7)
            softmax_recip(2)
            row_scale(0, 1, 8)
            row_scale(0, 1, 9)
            kv_bias(0)
            kv_bias(1)
            row_scale(0, 1, 10)
            normalize(0, 4)
            normalize(0, 5)
            k_elu(0)
            kv_bias(2)
            normalize(0, 6)
            normalize(0, 7)
            q_elu(0)
            k_elu(1)
            k_elu(2)
            kv_bias(3)
            turn_lo(0, 2)
            turn_lo(0, 3)
            kv_blocks(0)
            q_elu(1)
            k_elu(3)
            kv_bias(4)
            kv_bias(5)
            kv_blocks(1)
            attn_denominator(0)
            attn_recip(0)
            attn_denominator(1)
            attn_rows(0)
            attn_denominator(2)
            softmax_recip(3)
            attn_recip(1)
            attn_recip(2)
            attn_rows(1)
            attn_denominator(3)
            attn_recip(3)
            attn_rows(2)
            attn_rows(3)
            kv_bias(6)
            kv_bias(7)
            split_wo()
            add_output(0)
            k_elu(4)
            row_stats(1, 0)
            row_stats(1, 1)
            add_output(1)
            row_stats(1, 2)
            row_stats(1, 3)
            row_scale(1, 0, 0)
            k_elu(5)
            for i in range(1, 7):
                row_scale(1, 0, i)
            k_elu(6)
            row_scale(1, 0, 7)
            row_scale(1, 0, 8)
            k_elu(7)
            row_scale(1, 0, 9)
            q_elu(2)
            kv_blocks(2)
            row_scale(1, 0, 10)
            ln2_shift(0)
            q_elu(3)
            add_cross(0)
            row_stats(2, 0)
            row_stats(2, 1)
            add_cross(1)
            row_stats(2, 2)
            row_stats(2, 3)
            kv_blocks(3)
            row_scale(2, 0, 0)
            attn_denominator(4)
            attn_denominator(5)
            row_scale(2, 0, 1)
            attn_recip(4)
            row_scale(2, 0, 2)
            attn_recip(5)
            row_scale(2, 0, 3)
            attn_rows(4)
            row_scale(2, 0, 4)
            attn_rows(5)
            row_scale(2, 0, 5)
            attn_denominator(6)
            row_scale(2, 0, 6)
            attn_denominator(7)
            row_scale(2, 0, 7)
            attn_recip(6)
            row_scale(2, 0, 8)
            attn_recip(7)
            row_scale(2, 0, 9)
            attn_rows(6)
            row_scale(2, 0, 10)
            attn_rows(7)
            for i in range(0, 4):
                normalize(2, i)
            rows_lo("aT", 2)
            rows_lo("aT", 3)
            w2_low(0)
            turn_lo(2, 0)
            turn_lo(2, 1)
            w2_low(1)
            add_output(2)
            att_lo(2)
            add_output(3)
            att_lo(3)
            for i in range(4, 8):
                row_stats(1, i)
            hidden(0)
            for i in range(0, 7):
                row_scale(1, 1, i)
            rows_lo("lnT1", 2)
            row_scale(1, 1, 7)
            rows_lo("lnT1", 3)
            row_scale(1, 1, 8)
            w2_low(2)
            row_scale(1, 1, 9)
            row_scale(1, 1, 10)
            ln2_shift(1)
            hidden(1)
            hidden(2)
            add_cross(2)
            add_cross(3)
            for i in range(4, 8):
                row_stats(2, i)
            row_scale(2, 1, 0)
            row_scale(2, 1, 1)
            hidden(3)
            for i in range(2, 11):
                row_scale(2, 1, i)
            w2_low(3)
            for i in range(4, 8):
                normalize(2, i)
            hidden(4)
            hidden(5)
            turn_lo(2, 2)
            hidden(6)
            turn_lo(2, 3)
            hidden(7)
            hidden(8)
            output(0, 0)
            output(0, 1)
            output(1, 0)
            hidden(9)
            output(1, 1)
            for i in range(10, 16):
                hidden(i)
            hidden_lo(14)
            hidden_lo(15)
            output(2, 0)
            output(2, 1)
            output(3, 0)
            output(3, 1)

        @block.tensor
        def _(pe):
            def claim(*unit):
                if before[unit] is not None:
                    pe.wait_ge(*emptied(before[unit]))
                return bank[where[unit]]

            def raise_clock(n):
                ps = claim("clock", n)
                pe.wait_ge(zeroed, 1)
                for i in range(n):
                    last = nc.tensor.matmul(ps[:, 0:P], eq[:, 0, 0:P], eq[:, 0, 0:P], start=(i == 0), stop=(i == n - 1))
                last.then_inc(mm["clock"], 1)

            def cross_projection(n):
                h, which = n // 2, n % 2
                ps = claim("xqk", n)
                if n % 2 == 0:
                    pe.wait_ge(loaded[f"ctx{h}"], 16)
                    pe.wait_ge(loaded["wxqk"], 16)
                nc.tensor.matmul(ps[:, :], wxq[:, which, :], ctx_sb[:, h * N:(h + 1) * N],
                                 start=True, stop=True).then_inc(mm["xqk"], 1)

            def energy(b):
                ps = claim("energy", b)
                pe.wait_ge(xqk_done, 2 * (b // 2) + 2)
                for i in range(2):
                    last = nc.tensor.matmul(ps[:, i * S:(i + 1) * S], xqk[:, b, 0, i * P:(i + 1) * P], xqk[:, b, 1, :],
                                            start=True, stop=True)
                last.then_inc(mm["energy"], 1)

            def turn_rows(stage, g, i):
                rows, rows_done, step, first = {"lnT0": (ln, normed[0, g], 1, 0), "aT": (ln, attn_done, 1, g * TG),
                                                "lnT1": (res, x1_done, 2, g * TG), "lnT2": (ln, normed[2, g], 1, 0)}[stage]
                if i == 0:
                    pair = [claim(stage, 2 * g + c) for c in range(K)]
                else:
                    pair = [bank[where[stage, 2 * g + c]] for c in range(K)]
                if stage == "lnT0" and g == 0:
                    pe.wait_ge(loaded["cols"], 16)
                for t in (2 * i, 2 * i + 1):
                    if step == 1 or t % 2 == 0:
                        pe.wait_ge(rows_done, (first + t) // step + 1)
                    for c in range(K):
                        last = nc.tensor.transpose(pair[c][:, t * P:(t + 1) * P],
                                                   rows[:, g * TG + t, c * P:(c + 1) * P], ident)
                        if t == TG - 1:
                            last.then_inc(mm[stage], 1)

            def turn_att(b):
                ps = claim("attT", b)
                pe.wait_ge(att_done[b], 1)
                for k in range(K):
                    for i in range(2):
                        last = nc.tensor.transpose(ps[:, k * S + i * P:k * S + (i + 1) * P],
                                                   att[:, b, i, k * P:(k + 1) * P], ident)
                last.then_inc(mm["attT"], 1)

            def turned_in(layer, g, k, i):
                if i == 0:
                    pe.wait_ge(turned_hi[layer], 2 * g + k + 1)
                if i == 2:
                    pe.wait_ge(turned_lo[layer], 2 * g + k + 1)

            def query(n):
                g, m = n // 2, n % 2
                ps = claim("q", n)
                pe.wait_ge(wqkv_lo, 1)
                for i, (wp, xp) in enumerate(PARTS):
                    for k in range(K):
                        turned_in(0, g, k, i)
                        last = nc.tensor.matmul(ps[:, :], wqkv[wp][:, k, m * P:(m + 1) * P], lnT[xp][:, g, k, :],
                                                start=(i == 0 and k == 0), stop=(i == 2 and k == K - 1))
                last.then_inc(mm["q"], 1)

            def key_value(t):
                g, r = t // TG, t % TG
                ps = claim("kv", t)
                pe.wait_ge(wqkv_lo, 2)
                for i, (wp, xp) in enumerate(PARTS):
                    for k in range(K):
                        turned_in(0, g, k, i)
                        last = nc.tensor.matmul(ps[:, :], lnT[xp][:, g, k, r * P:(r + 1) * P], wqkv[wp][:, k, D:3 * D],
                                                start=(i == 0 and k == 0), stop=(i == 2 and k == K - 1))
                last.then_inc(mm["kv"], 1)

            def key_times_value(b):
                ps = claim("kvm", b)
                pe.wait_ge(k_done, 2 * b + 2)
                for c in range(K):
                    for i in range(2):
                        last = nc.tensor.matmul(ps[:, c * KVW:(c + 1) * KVW], kvs[:, 2 * b + i, c, 0:P],
                                                kvs[:, 2 * b + i, K + c, :], start=(i == 0), stop=(i == 1))
                last.then_inc(mm["kvm"], 1)

            def attention(t):
                g, r = t // TG, t % TG
                ps = claim("attn", t)
                pe.wait_ge(q_done, 2 * g + 2)
                pe.wait_ge(kvx_done, t // 2 + 1)
                W = P + HC
                for c in range(K):
                    last = nc.tensor.matmul(ps[:, c * W:(c + 1) * W], qp[:, g, c, r * P:(r + 1) * P],
                                            kvx[:, t // 2, c, :], start=True, stop=True)
                last.then_inc(mm["attn"], 1)

            def rows_times(stage, n, weights):
                ps = claim(stage, n)
                for i in range(2):
                    cols_t = slice((2 * (n % 2) + i) * P, (2 * (n % 2) + i + 1) * P)
                    steps = [(colT, weights(None, k), k) for k in range(K)] if n < 2 else \
                            [(colT1[xp], weights(wp, k), k) for wp, xp in PARTS for k in range(K)]
                    for m, (rows, w, k) in enumerate(steps):
                        last = nc.tensor.matmul(ps[:, i * D:(i + 1) * D], rows[:, k, cols_t], w,
                                                start=(m == 0), stop=(m == len(steps) - 1))
                last.then_inc(mm[stage], 1)

            def project(n):
                pe.wait_ge(loaded["ow"], 16)
                pe.wait_ge(aT_done, 2 * (n // 2) + 2)
                if n >= 2:
                    pe.wait_ge(aT_lo, 2)
                    pe.wait_ge(wo_lo, 1)
                rows_times("o", n, lambda part, k: wo[:, k, :] if part is None else wo_r[part][:, k, :])

            def cross(n):
                pe.wait_ge(turned2, 2 * (n // 2) + 2)
                pe.wait_ge(attT_done, n + 1)
                if n >= 2:
                    pe.wait_ge(turned2_lo, 2)
                    pe.wait_ge(attT_lo, n - 1)
                rows_times("xm", n, lambda part, k: attT[:, n, k, :] if part is None else attT1[part][:, n - 2, k, :])

            def hadamard(n):
                ps = claim("w2h", n)
                pe.wait_ge(ready, 1)
                pe.wait_ge(w2s_hi, n + 1)
                pe.wait_ge(w2s_lo, n + 1)
                for part in (1, 0):
                    last = nc.tensor.matmul(ps[:, :], had_r[:, :], w2s[part][:, n % 2, :, :].rearrange("p j d -> p (j d)"),
                                            start=(part == 1), stop=(part == 0))
                last.then_inc(mm["w2h"], 1)

            def up(i, which):
                g, j = i // J, i % J
                if i == 0:
                    pe.wait_ge(w13_hi, 4)
                    pe.wait_ge(w13_lo, 4)
                for which, stage in ((which, ("gate", "lin")[which]),):
                    ps = claim(stage, i)
                    for n, (wp, xp) in enumerate(PARTS):
                        for k in range(K):
                            if j == 0:
                                turned_in(2, g, k, n)
                            last = nc.tensor.matmul(ps[:, :], w13[wp][:, which, k, j * P:(j + 1) * P],
                                                    lnT[xp][:, g, k, :], start=(n == 0 and k == 0),
                                                    stop=(n == 2 and k == K - 1))
                    last.then_inc(mm[stage], 1)

            def down(i):
                g, j = i // J, i % J
                if j == 0:
                    for n in range(2):
                        claim("acc", 2 * g + n)
                if i == 0:
                    pe.wait_ge(w2_lo, 4)
                pe.wait_ge(hid_hi, i + 1)
                if i < G * J - LAST:
                    pe.wait_ge(hid_lo, i + 1)
                else:
                    pe.wait_ge(hid_lo_last, i - (G * J - LAST) + 1)
                for t in range(TG):
                    ps = bank[ACC[t // 2]][:, (t % 2) * D:(t % 2 + 1) * D]
                    for n, (wp, xp) in enumerate(PARTS):
                        last = nc.tensor.matmul(ps, hs[xp][:, i % 3, t * P:(t + 1) * P], w2[wp][:, j, :],
                                                start=(j == 0 and n == 0 and t % 2 == 0),
                                                stop=(j == J - 1 and n == 2 and t % 2 == 1), skip_group_check=True)
                    if j == J - 1 and t == 1:
                        last.then_inc(mm["acc"], 1)
                last.then_inc(mm["down"], 1)

            raise_clock(7)
            for i in range(0, 4):
                cross_projection(i)
            energy(0)
            energy(1)
            turn_rows("lnT0", 0, 0)
            turn_rows("lnT0", 0, 1)
            energy(2)
            energy(3)
            key_value(0)
            query(0)
            for i in range(1, 4):
                key_value(i)
            turn_rows("lnT0", 1, 0)
            query(1)
            turn_rows("lnT0", 1, 1)
            turn_att(0)
            key_times_value(0)
            key_value(4)
            key_value(5)
            key_times_value(1)
            for i in range(0, 4):
                attention(i)
            key_value(6)
            turn_rows("aT", 0, 0)
            turn_rows("aT", 0, 1)
            turn_att(1)
            key_value(7)
            project(0)
            project(1)
            turn_rows("lnT1", 0, 0)
            query(2)
            turn_rows("lnT1", 0, 1)
            query(3)
            key_times_value(2)
            cross(0)
            cross(1)
            key_times_value(3)
            for i in range(4, 8):
                attention(i)
            turn_rows("aT", 1, 0)
            hadamard(0)
            turn_att(2)
            turn_att(3)
            turn_rows("aT", 1, 1)
            turn_rows("lnT2", 0, 0)
            turn_rows("lnT2", 0, 1)
            hadamard(1)
            hadamard(2)
            project(2)
            up(0, 0)
            project(3)
            turn_rows("lnT1", 1, 0)
            up(0, 1)
            turn_rows("lnT1", 1, 1)
            up(1, 0)
            up(1, 1)
            up(2, 0)
            up(2, 1)
            cross(2)
            up(3, 0)
            cross(3)
            hadamard(3)
            up(3, 1)
            up(4, 0)
            up(4, 1)
            up(5, 0)
            up(5, 1)
            turn_rows("lnT2", 1, 0)
            turn_rows("lnT2", 1, 1)
            down(0)
            up(6, 0)
            down(1)
            up(6, 1)
            down(2)
            down(3)
            up(7, 0)
            up(7, 1)
            up(8, 0)
            for i in range(4, 7):
                down(i)
            up(8, 1)
            down(7)
            up(9, 0)
            up(9, 1)
            up(10, 0)
            up(10, 1)
            up(11, 0)
            down(8)
            up(11, 1)
            up(12, 0)
            up(12, 1)
            up(13, 0)
            down(9)
            up(13, 1)
            up(14, 0)
            up(14, 1)
            down(10)
            down(11)
            up(15, 0)
            up(15, 1)
            for i in range(12, 16):
                down(i)


def kernel(**inputs):
    import numpy as np
    import concourse.bacc as bacc
    from concourse.bass_utils import run_bass_kernel_spmd

    P, HD, D = 128, 16, 256
    ones = np.ones((1, 1), np.float32)
    had = ones
    while had.shape[0] < P:
        had = np.block([[had, had], [had, -had]])
    heads = np.arange(P) // HD
    a = {n: np.asarray(v) for n, v in inputs.items()}
    cols = np.concatenate([
        np.eye(P, dtype=np.float32), had.astype(np.float32),
        (heads[:, None] == heads[None, :]).astype(np.float32),
        (heads[:, None] == np.arange(P // HD)[None, :]).astype(np.float32),
        a["L0_attn_q_b"].reshape(-1, P).T, a["L0_xattn_bq"].reshape(P, 1), a["L0_xattn_bk"].reshape(P, 1)], axis=1)
    arrays = {
        "x": a["x"].reshape(-1, D),
        "ctxT": a["ctx_1024"].reshape(-1, P).T,
        "q_wT": a["L0_attn_q_w"].T,
        "kv_wT": np.concatenate([a["L0_attn_k_w"].T, a["L0_attn_v_w"].T], axis=1),
        "o_wT": a["L0_attn_o_w"].T,
        "xqk_wT": np.concatenate([a["L0_xattn_Wq"].T, a["L0_xattn_Wk"].T], axis=1),
        "w1T": a["L0_ffn_W1"].T, "w3T": a["L0_ffn_W3"].T, "w2T": a["L0_ffn_W2"].T,
        "row_bias": np.concatenate([a["L0_attn_k_b"], a["L0_attn_v_b"], a["L0_attn_o_b"]]),
        "cols": cols,
    }
    arrays = {n: np.ascontiguousarray(v) for n, v in arrays.items()}
    nc = bacc.Bacc("TRN2", target_bir_lowering=False, num_devices=1)
    aps = [nc.dram_tensor(n, v.shape, mybir.dt.float32, kind="ExternalInput").ap() for n, v in arrays.items()]
    out = nc.dram_tensor("out", (a["x"].size // D, D), mybir.dt.float32, kind="ExternalOutput").ap()
    decoder_layer(nc, *aps, out)
    r = run_bass_kernel_spmd(nc, [arrays], core_ids=[0])
    return r.results[0]["out"].reshape(a["x"].shape)
```
